# Optimizing a Trainium2 kernel written in Bass

```python
import numpy as np
import jax
import jax.numpy as jnp

def _softmax(x, axis=-1):
    return jax.nn.softmax(x, axis=axis)

def _gelu(x):
    return jax.nn.gelu(x, approximate=True)

def _silu(x):
    return jax.nn.silu(x)

def _sigmoid(x):
    return jax.nn.sigmoid(x)

def _layernorm(x, axis=-1, eps=1e-05):
    m = jnp.mean(x, axis=axis, keepdims=True)
    v = jnp.var(x, axis=axis, keepdims=True)
    return (x - m) / jnp.sqrt(v + eps)

def _scatter_add(tgt, idx, src, axis=0):
    return tgt.at[idx].add(src)

def _segment_sum(src, seg, n):
    return jax.ops.segment_sum(src, seg, n)
kernel_name = 'mk_seq_postln_d1_jaxref_r8_26aad3'

def setup_inputs(seed: int=0):
    np.random.seed(seed)
    _w = jnp.asarray

    def _L0_attn_setup():
        import jax, jax.numpy as jnp
        import numpy as np
        import math
        NUM_HEADS = 8
        D_HEAD = 128
        DEPTH = 1
        LAMBDA_INIT = 0.8 - 0.6 * math.exp(-0.3 * DEPTH)
        EPS = 1e-05
        key = jax.random.key(seed)
        ks = jax.random.split(key, 10)
        B, N, D = (2, 256, 128)
        s = 0.02
        return {'X': jax.random.normal(ks[0], (B, N, D), jnp.float32), 'Wq': jax.random.normal(ks[1], (2 * D_HEAD * NUM_HEADS, D), jnp.float32) * s, 'Wk': jax.random.normal(ks[2], (2 * D_HEAD * NUM_HEADS, D), jnp.float32) * s, 'Wv': jax.random.normal(ks[3], (2 * D_HEAD * NUM_HEADS, D), jnp.float32) * s, 'Wo': jax.random.normal(ks[4], (D, 2 * D_HEAD * NUM_HEADS), jnp.float32) * s, 'lambda_q1': jax.random.normal(ks[5], (NUM_HEADS, D_HEAD), jnp.float32) * 0.1, 'lambda_k1': jax.random.normal(ks[6], (NUM_HEADS, D_HEAD), jnp.float32) * 0.1, 'lambda_q2': jax.random.normal(ks[7], (NUM_HEADS, D_HEAD), jnp.float32) * 0.1, 'lambda_k2': jax.random.normal(ks[8], (NUM_HEADS, D_HEAD), jnp.float32) * 0.1, 'rms_scale': jnp.ones((2 * D_HEAD,), jnp.float32)}
    _L0_attn_in = _L0_attn_setup()

    def _L0_ffn_setup():
        import jax, jax.numpy as jnp
        import numpy as np
        NUM_EXPERTS = 8
        EXPERT_CAPACITY = 2.0
        key = jax.random.key(seed)
        k1, k2, k3, k4 = jax.random.split(key, 4)
        B, T, C, H, E = (4, 512, 128, 512, NUM_EXPERTS)
        x = jax.random.normal(k1, (B, T, C), jnp.float32)
        gate_w = jax.random.normal(k2, (C, E), jnp.float32) * 0.02
        w1 = jax.random.normal(k3, (E, C, H), jnp.float32) * 0.02
        w2 = jax.random.normal(k4, (E, H, C), jnp.float32) * 0.02
        return {'x': x, 'gate_w': gate_w, 'w1': w1, 'w2': w2}
    _L0_ffn_in = _L0_ffn_setup()
    _d = {'L0_attn_X': _L0_attn_in['X'], 'L0_attn_Wq': _L0_attn_in['Wq'], 'L0_attn_Wk': _L0_attn_in['Wk'], 'L0_attn_Wv': _L0_attn_in['Wv'], 'L0_attn_Wo': _L0_attn_in['Wo'], 'L0_attn_lambda_q1': _L0_attn_in['lambda_q1'], 'L0_attn_lambda_k1': _L0_attn_in['lambda_k1'], 'L0_attn_lambda_q2': _L0_attn_in['lambda_q2'], 'L0_attn_lambda_k2': _L0_attn_in['lambda_k2'], 'L0_attn_rms_scale': _L0_attn_in['rms_scale'], 'L0_ffn_gate_w': _L0_ffn_in['gate_w'], 'L0_ffn_w1': _L0_ffn_in['w1'], 'L0_ffn_w2': _L0_ffn_in['w2']}
    _x0 = _d['L0_attn_X']
    _d['L0_attn_X'] = jax.random.normal(jax.random.fold_in(jax.random.key(seed), 1), (2, 1024, 128), dtype=_x0.dtype)
    del _x0
    return _d

def reference(L0_attn_X, L0_attn_Wq, L0_attn_Wk, L0_attn_Wv, L0_attn_Wo, L0_attn_lambda_q1, L0_attn_lambda_k1, L0_attn_lambda_q2, L0_attn_lambda_k2, L0_attn_rms_scale, L0_ffn_gate_w, L0_ffn_w1, L0_ffn_w2):

    def _L0_attn_ref(X, Wq, Wk, Wv, Wo, lambda_q1, lambda_k1, lambda_q2, lambda_k2, rms_scale):
        import jax, jax.numpy as jnp
        import numpy as np
        import math
        NUM_HEADS = 8
        D_HEAD = 128
        DEPTH = 1
        LAMBDA_INIT = 0.8 - 0.6 * math.exp(-0.3 * DEPTH)
        EPS = 1e-05
        B, N, D = X.shape
        H, dh = (NUM_HEADS, D_HEAD)

        def proj(W):
            y = jnp.einsum('bnd,ed->bne', X, W)
            return y.reshape(B, N, H, 2 * dh).transpose(0, 2, 1, 3)
        Q = proj(Wq)
        K = proj(Wk)
        V = proj(Wv)
        Q1, Q2 = (Q[..., :dh], Q[..., dh:])
        K1, K2 = (K[..., :dh], K[..., dh:])
        lam1 = jnp.exp(jnp.sum(lambda_q1 * lambda_k1, axis=-1))
        lam2 = jnp.exp(jnp.sum(lambda_q2 * lambda_k2, axis=-1))
        lam = (lam1 - lam2 + LAMBDA_INIT)[None, :, None, None]
        scaling = 1.0 / math.sqrt(dh)
        A1 = jnp.einsum('bhqd,bhkd->bhqk', Q1, K1) * scaling
        A2 = jnp.einsum('bhqd,bhkd->bhqk', Q2, K2) * scaling
        attn = jax.nn.softmax(A1, axis=-1) - lam * jax.nn.softmax(A2, axis=-1)
        O = jnp.einsum('bhqk,bhkd->bhqd', attn, V)
        rms = jnp.sqrt(jnp.mean(O * O, axis=-1, keepdims=True) + EPS)
        O = O / rms * rms_scale
        O = O * (1.0 - LAMBDA_INIT)
        O = O.transpose(0, 2, 1, 3).reshape(B, N, H * 2 * dh)
        return jnp.einsum('bne,de->bnd', O, Wo)

    def _L0_ffn_ref(x, gate_w, w1, w2):
        import jax, jax.numpy as jnp
        import numpy as np
        NUM_EXPERTS = 8
        EXPERT_CAPACITY = 2.0
        B, T, C = x.shape
        E = gate_w.shape[1]
        cap = int(EXPERT_CAPACITY * T / E)
        scores = jnp.einsum('BTC,CE->BTE', x, gate_w)
        probs = jax.nn.softmax(scores, axis=-1)
        probs_et = jnp.transpose(probs, (0, 2, 1))
        top_p, top_idx = jax.lax.top_k(probs_et, cap)
        xin = jnp.take_along_axis(x[:, None, :, :], top_idx[..., None], axis=2)
        h = jax.nn.gelu(jnp.einsum('BElC,ECH->BElH', xin, w1), approximate=False)
        y = jnp.einsum('BElH,EHC->BElC', h, w2)
        y = y * top_p[..., None]
        b_idx = jnp.arange(B)[:, None, None]
        out = jnp.zeros((B, T, C), x.dtype).at[b_idx, top_idx].add(y)
        return out
    x = L0_attn_X
    x = _layernorm(x + _L0_attn_ref(x, L0_attn_Wq, L0_attn_Wk, L0_attn_Wv, L0_attn_Wo, L0_attn_lambda_q1, L0_attn_lambda_k1, L0_attn_lambda_q2, L0_attn_lambda_k2, L0_attn_rms_scale), axis=-1)
    x = _layernorm(x + _L0_ffn_ref(x, L0_ffn_gate_w, L0_ffn_w1, L0_ffn_w2), axis=-1)
    return x

_drawn_inputs = setup_inputs


def setup_inputs(seed=0):
    import zlib

    import numpy as np

    out = dict(_drawn_inputs(seed))
    spreads = {'L0_attn_rms_scale': (1.0, 0.2)}
    factors = {'L0_attn_lambda_k2': 3.025, 'L0_ffn_gate_w': 5.373, 'L0_ffn_w1': 4.805, 'L0_ffn_w2': 4.739}
    for name, (base, spread) in spreads.items():
        noise = np.random.default_rng([zlib.crc32(name.encode()), seed]).standard_normal(out[name].shape)
        drawn = base * np.exp(spread * noise) if base else spread * noise
        out[name] = jnp.asarray(drawn.astype(out[name].dtype))
    for name, factor in factors.items():
        out[name] = (out[name] * factor).astype(out[name].dtype)
    return out
```

```python
import concourse.bass as bass
from concourse import mybir
from contextlib import ExitStack
import math

F32 = mybir.dt.float32
F32R = mybir.dt.float32r
I32 = mybir.dt.int32
ALU = mybir.AluOpType
ACT = mybir.ActivationFunctionType
AX = mybir.AxisListType


def need(eng, sem, value):
    if isinstance(value, int) and value <= 0:
        return
    eng.wait_ge(sem, value)


def build(nc, X, Wq, Wk, Wv, Wo, lq1, lk1, lq2, lk2, rms_scale, gate_w, w1, w2, out):
    B, N, D = X.shape
    H, DH = lq1.shape
    DV = 2 * DH
    E = gate_w.shape[1]
    F = w1.shape[2]
    P = 128
    QT = N // P
    KT = N // P
    TPH = B * QT
    GT = 4
    GPH = TPH // GT
    NC = 512
    NCH = N // NC
    CAP = int(2.0 * N / E)
    LAMBDA_INIT = 0.8 - 0.6 * math.exp(-0.3)
    SCALE = 1.0 / math.sqrt(DH)
    EPS = 1e-5
    WWN = DV + D

    FT = F // P
    R = B * E
    REP = P // R
    LB = REP.bit_length() - 1
    LEVELS = 30 // LB

    LAG_T = 1
    LAG_U = 6
    LAG_O = 10
    LAG_Y = 11
    AT_QB, AT_WT, AT_WP, AT_M, AT_QA = (1, 2), 4, 6, 9, (11, 13)
    AT_WW = 10

    ctx = ExitStack()
    with ctx:
        def sb(name, shape, dt=F32):
            return ctx.enter_context(nc.sbuf_tensor(name, shape, dt))

        def ps(name, shape, dt=F32):
            return ctx.enter_context(nc.psum_tensor(name, shape, dt))

        def sem(name):
            return ctx.enter_context(nc.semaphore(name))

        xres = sb("xres", [P, TPH, D])
        xk_hi = sb("xk_hi", [P, TPH, D], F32R)
        xk_lo = sb("xk_lo", [P, TPH, D], F32R)
        xt_hi = sb("xt_hi", [P, B * N], F32R)
        xt_lo = sb("xt_lo", [P, B * N], F32R)
        q_hi = sb("q_hi", [P, B, 2, N], F32R)
        q_lo = sb("q_lo", [P, B, 2, N], F32R)
        prob = sb("prob", [P, 2, 2, N])
        attn = sb("attn", [P, 2, N])
        at32 = sb("at32", [P, 2, N])
        at_hi = sb("at_hi", [P, 2, KT, NC], F32R)
        at_lo = sb("at_lo", [P, 2, KT, NC], F32R)
        u_hi = sb("u_hi", [P, NC], F32R)
        u_lo = sb("u_lo", [P, NC], F32R)
        wq_s = sb("wq_s", [P, 2, D])
        wk_s = sb("wk_s", [P, 2, D])
        wv_s = sb("wv_s", [P, 2, D])
        wo_s = sb("wo_s", [P, DV])
        wot_s = sb("wot_s", [P, 2, D])
        m_hi = sb("m_hi", [P, 2, D], F32R)
        m_lo = sb("m_lo", [P, 2, D], F32R)
        wwn_hi = sb("wwn_hi", [P, WWN], F32R)
        wwn_lo = sb("wwn_lo", [P, WWN], F32R)
        ww_hi = sb("ww_hi", [P, WWN], F32R)
        ww_lo = sb("ww_lo", [P, WWN], F32R)
        rms_c = sb("rms_c", [P, 2])
        rms_raw = sb("rms_raw", [P, 2])
        ident = sb("ident", [P, P])
        ones = sb("ones", [P, P])
        neg_half = sb("neg_half", [P, TPH])
        lam_in = sb("lam_in", [H, 4, DH])
        lam_pr = sb("lam_pr", [H, 2, DH])
        lam_s = sb("lam_s", [H, 4])
        lam_d = sb("lam_d", [H, H])
        neglam = sb("neglam", [P, H])
        neglam_h = sb("neglam_h", [P, 1])
        negmax = sb("negmax", [P, 2, 2])
        psum1 = sb("psum1", [P, TPH])
        psum2 = sb("psum2", [P, 2])
        rs2 = sb("rs2", [P, 2])
        coef = sb("coef", [P, 2])
        osq = sb("osq", [P, 2, DV])
        ssq = sb("ssq", [P, 2])
        es1 = sb("es1", [P, 2])
        s1sq = sb("s1sq", [P, TPH])
        eps_c = sb("eps_c", [P, 1])
        var_o = sb("var_o", [P, 2])
        fac = sb("fac", [P, 2])

        x1 = xres
        x1t = prob[:, 0].rearrange("p m n -> p (m n)")
        acc_t = prob[:, 1].rearrange("p m n -> p (m n)")
        sq = attn[:, :, :].rearrange("p a n -> p (a n)").rearrange("p (t d) -> p t d", d=D)
        gelu = attn
        w1_raw = at32[:, 0, 0:F]
        w2_raw = at32[:, 0, F:2 * F]
        prod = at32[:, 1, :]
        w1_hi = xk_hi[:, 0:FT, :]
        w1_lo = xk_lo[:, 0:FT, :]
        w2_hi = xk_hi[:, FT:2 * FT, :]
        w2_lo = xk_lo[:, FT:2 * FT, :]
        g_hi = at_hi[:, :, :, :].rearrange("p b (f c) n -> p b f c n", c=NCH)
        g_lo = at_lo[:, :, :, :].rearrange("p b (f c) n -> p b f c n", c=NCH)
        weights = sb("weights", [P, B * N])
        tick = sb("tick", [P, B, FT])
        gate_s = sb("gate_s", [D, E])
        stat = sb("stat", [P, 4, TPH])
        ln_eps = sb("ln_eps", [P, TPH])
        pr = sb("pr", [P, QT, R])
        pst = sb("pst", [P, 3, TPH])
        p_rows = weights[0:R, 0:N]
        rows = weights[:, N:2 * N]
        tie, cum = prob[:, 1, 0, :], prob[:, 1, 1, :]
        sel = sb("sel", [R, P])
        grp = sb("grp", [P, P])
        base = sb("base", [P, 1], I32)
        cand = sb("cand", [P, 1], I32)
        jcur = sb("jcur", [P, 1], I32)
        step = sb("step", [P, 1], I32)
        pw = sb("pw", [P, 1])
        cnt = sb("cnt", [P, 1])
        hit = sb("hit", [P, 1])
        cnt_gt = sb("cnt_gt", [P, 1])
        free_n = sb("free_n", [P, 1])
        w_dram = nc.dram_tensor("w_dram", (R, N), F32).ap()

        ring = [ps("ring_a", [P, N]), ps("ring_b", [P, N])]
        t_ps = ps("t_ps", [P, N])
        u_ps = ps("u_ps", [P, NC])
        o_ps = ps("o_ps", [P, NC])

        x_in = [sem(f"x_in{b}") for b in range(B)]
        qk_in, vo_in, lam_in_s, rms_in = sem("qk_in"), sem("vo_in"), sem("lam_in_s"), sem("rms_in")
        const_ready = sem("const_ready")
        xt_ready, xt_hi_done, xt_split = sem("xt_ready"), sem("xt_hi_done"), sem("xt_split")
        xk_hi_done, xk_split = sem("xk_hi_done"), sem("xk_split")
        lam_prod, lam_sum, lam_exp, lam_diag, lam_ps = (
            sem("lam_prod"), sem("lam_sum"), sem("lam_exp"), sem("lam_diag"), sem("lam_ps"))
        lam_ready, lam_head, rms_ready = sem("lam_ready"), sem("lam_head"), sem("rms_ready")
        m_ready, m_hi_done, m_split = sem("m_ready"), sem("m_hi_done"), sem("m_split")
        q_ready, q_hi_done, q_split = sem("q_ready"), sem("q_hi_done"), sem("q_split")
        wt_ready, wt_hi_done, wt_split = sem("wt_ready"), sem("wt_hi_done"), sem("wt_split")
        wp_ready, wp_hi_done, wp_split, ww_installed = (
            sem("wp_ready"), sem("wp_hi_done"), sem("wp_split"), sem("ww_installed"))
        scores_ready, negmax_ready, prob_ready = sem("scores_ready"), sem("negmax_ready"), sem("prob_ready")
        rs2_ready, coef_ready, attn_ready = sem("rs2_ready"), sem("coef_ready"), sem("attn_ready")
        t_ready, t_copied, at_hi_done, at_split = sem("t_ready"), sem("t_copied"), sem("at_hi_done"), sem("at_split")
        u_ready, u_hi_done, u_split = sem("u_ready"), sem("u_hi_done"), sem("u_split")
        s1sq_ready = sem("s1sq_ready")
        o_ready, ssq_ready, es1_ready, var_ready, fac_ready, y_added = (
            sem("o_ready"), sem("ssq_ready"), sem("es1_ready"), sem("var_ready"), sem("fac_ready"), sem("y_added"))
        out_done = sem("out_done")
        eps_ready, ln_sum, ln_mean, ln_cent, ln_sq, ln_ssq, ln_var, ln_fac, ln_done = (
            sem("eps_ready"), sem("ln_sum"), sem("ln_mean"), sem("ln_cent"), sem("ln_sq"), sem("ln_ssq"),
            sem("ln_var"), sem("ln_fac"), sem("ln_done"))
        gate_in, x1t_ready, x1t_copied, x1t_hi_done, x1t_split, acc_ready = (
            sem("gate_in"), sem("x1t_ready"), sem("x1t_copied"), sem("x1t_hi_done"), sem("x1t_split"),
            sem("acc_ready"))
        gate_ready, gate_step, gate_exp, prows_ready, prows_copied, rows_ready, rows_copied = (
            sem("gate_ready"), sem("gate_step"), sem("gate_exp"), sem("prows_ready"), sem("prows_copied"),
            sem("rows_ready"), sem("rows_copied"))
        sel_ready, base_ready, cand_ready, cnt_ready, hit_ready, votes_ready, step_ready = (
            sem("sel_ready"), sem("base_ready"), sem("cand_ready"), sem("cnt_ready"), sem("hit_ready"),
            sem("votes_ready"), sem("step_ready"))
        next_ready, tie_step, w_stored, w_in = (
            sem("next_ready"), sem("tie_step"), sem("w_stored"), [sem("w_in0"), sem("w_in1")])
        w1_in, w2_in, w1_hi_done, w1_split, w2_hi_done, w2_split = (
            sem("w1_in"), sem("w2_in"), sem("w1_hi_done"), sem("w1_split"), sem("w2_hi_done"), sem("w2_split"))
        up_ready, gelu_ready, g_hi_done, g_split, down_ready, prod_ready, acc_added = (
            sem("up_ready"), sem("gelu_ready"), sem("g_hi_done"), sem("g_split"), sem("down_ready"),
            sem("prod_ready"), sem("acc_added"))
        back_ready, back_copied, ticked = sem("back_ready"), sem("back_copied"), sem("ticked")

        def q_index(h, which, m):
            return 4 * h + (2 if which == "b" else 0) + m

        def exists(h, r, first):
            return not (first and r < 0)

        block = ctx.enter_context(nc.Block())

        def heads(eng, slot):
            for i in range(TPH):
                slot(0, i, True, False, False)
            with eng.Fori(1, H - 1) as h:
                for i in range(TPH):
                    slot(h, i, False, False, False)
            for i in range(TPH):
                slot(H - 1, i, False, True, False)
            for i in range(TPH, TPH + LAG_Y):
                slot(H - 1, i, False, True, True)

        def experts(eng, step_of):
            step_of(0, True, False)
            with eng.Fori(1, E - 1) as e:
                step_of(e, False, False)
            step_of(E - 1, False, False)
            step_of(E, False, True)

        @block.sync
        def _(sp):
            for b in range(B):
                sp.dma_start(xres[:, b * QT:(b + 1) * QT, :],
                             X[b].rearrange("(t p) d -> p t d", p=P)).then_inc(x_in[b], 16)
            wq_v = Wq.rearrange("(h m e) d -> h e m d", m=2, e=P)
            wk_v = Wk.rearrange("(h m e) d -> h e m d", m=2, e=P)
            wv_v = Wv.rearrange("(h m e) d -> h e m d", m=2, e=P)
            wo_v = Wo.rearrange("d (h e) -> h d e", e=DV)

            def load_qk(h):
                sp.dma_start(wq_s[:, :, :], wq_v[bass.ds(h, 1)].rearrange("a e m d -> (a e) m d")).then_inc(qk_in, 16)
                sp.dma_start(wk_s[:, :, :], wk_v[bass.ds(h, 1)].rearrange("a e m d -> (a e) m d")).then_inc(qk_in, 16)

            def load_vo(h):
                sp.dma_start(wv_s[:, :, :], wv_v[bass.ds(h, 1)].rearrange("a e m d -> (a e) m d")).then_inc(vo_in, 16)
                sp.dma_start(wo_s[:, :], wo_v[bass.ds(h, 1)].rearrange("a d e -> (a d) e")).then_inc(vo_in, 16)

            load_qk(0)
            load_vo(0)
            for n, v in enumerate((lq1, lk1, lq2, lk2)):
                sp.dma_start(lam_in[:, n, :], v).then_inc(lam_in_s, 16)
            with nc.allow_non_contiguous_dma(reason="256 numbers, once"):
                sp.dma_start(rms_raw[:, :], rms_scale.rearrange("(m e) -> e m", e=P)).then_inc(rms_in, 16)
            with sp.Fori(1, H) as h:
                sp.wait_ge(m_ready, h)
                load_qk(h)
                sp.wait_ge(wp_ready, h)
                load_vo(h)
            sp.dma_start(gate_s[:, :], gate_w).then_inc(gate_in, 16)
            w2_v = w2.rearrange("e (f p) c -> e p f c", p=P)

            def load_w1(e):
                sp.dma_start(w1_raw, w1[bass.ds(e, 1)].rearrange("a c f -> (a c) f")).then_inc(w1_in, 16)

            def load_w2(e):
                sp.dma_start(w2_raw.rearrange("p (f c) -> p f c", f=FT),
                             w2_v[bass.ds(e, 1)].rearrange("a p f c -> (a p) f c")).then_inc(w2_in, 16)

            def load_weights(e, b):
                src = w_dram.rearrange("(b e) n -> b e n", b=B)[b][bass.ds(e, 1), :]
                sp.dma_start(weights[:, b * N:(b + 1) * N],
                             src.rearrange("a n -> (a n)").partition_broadcast(P)).then_inc(w_in[b], 16)

            sp.wait_ge(at_split, H * TPH)
            load_w1(0)
            load_w2(0)
            sp.wait_ge(tie_step, 7)
            sp.dma_start(w_dram, rows[0:P:REP, :]).then_inc(w_stored, 16)
            sp.wait_ge(w_stored, 16)
            for b in range(B):
                load_weights(0, b)
            with sp.Fori(0, E - 1) as e:
                sp.wait_ge(w1_split, e + 1)
                load_w1(e + 1)
                sp.wait_ge(w2_split, e + 1)
                load_w2(e + 1)
                for b in range(B):
                    sp.wait_ge(prod_ready, 2 * e + b + 1)
                    load_weights(e + 1, b)
            for b in range(B):
                sp.wait_ge(ln_done, B + b + 1)
                sp.dma_start(out[b].rearrange("(t p) d -> p t d", p=P),
                             x1[:, b * QT:(b + 1) * QT, :]).then_inc(out_done, 16)
            sp.wait_ge(out_done, 16 * B)

        @block.gpsimd
        def _(pool):
            pool.memset(ident[:, :], 0.0).then_inc(const_ready, 1)
            pool.memset(ones[:, :], 1.0).then_inc(const_ready, 1)
            pool.memset(neg_half[:, :], -0.5).then_inc(const_ready, 1)
            pool.memset(eps_c[:, :], EPS * DV).then_inc(const_ready, 1)
            pool.wait_ge(const_ready, 4)
            pool.affine_select(out=ident[:, :], in_=ident[:, :], compare_op=ALU.not_equal, fill=1.0, base=0,
                               pattern=[[-1, P]], channel_multiplier=1).then_inc(const_ready, 1)
            for b in range(B):
                pool.wait_ge(xk_hi_done, b + 1)
                s = slice(b * QT, (b + 1) * QT)
                pool.tensor_tensor(xk_lo[:, s, :], xres[:, s, :], xk_hi[:, s, :].bitcast(F32),
                                   ALU.subtract).then_inc(xk_split, 1)

            def slot(h, i, first, last, tail):
                t = TPH * h + i
                r = i - LAG_O
                if exists(h, r, first) and r < TPH:
                    tt, par = t - LAG_O, r % 2
                    pool.wait_ge(s1sq_ready, tt + 1)
                    need(pool, var_ready, tt - 1)
                    pool.tensor_tensor(es1[:, par:par + 1], s1sq[:, r % TPH:r % TPH + 1], eps_c[:, 0:1],
                                       ALU.mult).then_inc(es1_ready, 1)
                    pool.wait_ge(es1_ready, tt + 1)
                    pool.wait_ge(ssq_ready, tt + 1)
                    pool.tensor_tensor(var_o[:, par:par + 1], ssq[:, par:par + 1], es1[:, par:par + 1],
                                       ALU.add).then_inc(var_ready, 1)
                    need(pool, y_added, tt - 1)
                    pool.wait_ge(var_ready, tt + 1)
                    pool.tensor_tensor(fac[:, par:par + 1], var_o[:, par:par + 1], neg_half[:, 0:1],
                                       ALU.pow).then_inc(fac_ready, 1)
                r = i - LAG_T
                if exists(h, r, first) and r < TPH:
                    tt, par, g = t - LAG_T, r % 2, (r // GT) % 2
                    need(pool, t_copied, tt + 1)
                    gabs = GPH * h + r // GT
                    if not (first and r // GT < 2):
                        pool.wait_ge(u_ready, gabs - 1)
                    s1 = psum1[:, r % TPH:r % TPH + 1]
                    pool.tensor_tensor(s1sq[:, r % TPH:r % TPH + 1], s1, s1, ALU.mult).then_inc(s1sq_ready, 1)
                    c = slice((r % GT) * P, (r % GT + 1) * P)
                    src = at32[:, par, :].rearrange("p (k q) -> p k q", q=P)
                    pool.tensor_scalar(at_hi[:, g, :, c], src, 1.0, 0.0, ALU.mult, ALU.add).then_inc(at_hi_done, 1)
                    pool.wait_ge(at_hi_done, tt + 1)
                    pool.tensor_tensor(at_lo[:, g, :, c], src, at_hi[:, g, :, c].bitcast(F32),
                                       ALU.subtract).then_inc(at_split, 1)

            heads(pool, slot)

            def ln_factors(n):
                c = slice((n % B) * QT, (n % B + 1) * QT)
                pool.wait_ge(ln_ssq, n + 1)
                pool.tensor_tensor(stat[:, 1, c], stat[:, 1, c], ln_eps[:, c], ALU.add).then_inc(ln_var, 1)
                pool.wait_ge(ln_var, n + 1)
                pool.tensor_tensor(stat[:, 2, c], stat[:, 1, c], neg_half[:, c], ALU.pow).then_inc(ln_fac, 1)

            pool.memset(ln_eps[:, :], EPS * D).then_inc(eps_ready, 1)
            pool.wait_ge(eps_ready, 1)
            pool.memset(sel[:, :], 1.0).then_inc(sel_ready, 1)
            pool.memset(grp[:, :], 1.0).then_inc(sel_ready, 1)
            pool.memset(base[:, :], 0).then_inc(sel_ready, 1)
            pool.memset(pw[:, :], float(2 ** (LB * (LEVELS - 1)))).then_inc(sel_ready, 1)
            pool.iota(jcur[:, :], pattern=[[0, 1]], base=0, channel_multiplier=1).then_inc(sel_ready, 1)
            for n, (buf, pat, mult) in enumerate((
                    (sel[:, :], [[1, P]], -REP),
                    (grp[:, :].rearrange("p (g j) -> p g j", j=REP), [[-REP, R], [0, REP]], 1))):
                pool.wait_ge(sel_ready, 5 + 2 * n)
                pool.affine_select(out=buf, in_=buf, compare_op=ALU.is_ge, fill=0.0, base=0, pattern=pat,
                                   channel_multiplier=mult).then_inc(sel_ready, 1)
                pool.wait_ge(sel_ready, 6 + 2 * n)
                pool.affine_select(out=buf, in_=buf, compare_op=ALU.is_ge, fill=0.0, base=REP - 1,
                                   pattern=[[-a, c] for a, c in pat], channel_multiplier=-mult).then_inc(sel_ready, 1)
            for n in range(B):
                ln_factors(n)

            def g_round(e, b):
                for f in range(FT):
                    n = 2 * FT * e + FT * b + f
                    pool.wait_ge(gelu_ready, n + 1)
                    if f == 0:
                        need(pool, down_ready, 2 * (e - 1) + b + 1)
                    pool.tensor_tensor(tick[:, b, f:f + 1], eps_c[:, 0:1], eps_c[:, 0:1],
                                       ALU.mult).then_inc(ticked, 1)
                    pool.tensor_scalar(g_hi[:, b, f, :, :], gelu[:, f % 2, :].rearrange("p (c n) -> p c n", c=NCH),
                                       1.0, 0.0, ALU.mult, ALU.add).then_inc(g_hi_done, 1)

            def ffn(e, first, tail):
                if not tail:
                    for b in range(B):
                        g_round(e, b)

            experts(pool, ffn)
            for n in range(B, 2 * B):
                ln_factors(n)

        @block.scalar
        def _(act):
            for b in range(B):
                act.wait_ge(xt_ready, b + 1)
                act.activation(xt_hi[:, b * N:(b + 1) * N], ring[b][:, :], ACT.Copy).then_inc(xt_hi_done, 1)
            def q_round(h, which, maps=(0, 1)):
                for m in maps:
                    b = 1 if which == "b" else 0
                    for c in range(NCH):
                        cols = slice(c * NC, (c + 1) * NC)
                        act.wait_ge(q_ready, NCH * q_index(h, which, m) + c + 1)
                        act.activation(q_hi[:, b, m, cols], ring[m][:, cols], ACT.Copy).then_inc(q_hi_done, 1)

            q_round(0, "a")
            act.wait_ge(lam_sum, 2)
            act.activation(lam_s[:, 2:4], lam_s[:, 0:2], ACT.Exp).then_inc(lam_exp, 1)

            def slot(h, i, first, last, tail):
                t = TPH * h + i

                def q_rounds(m):
                    if not tail and i == AT_QB[m]:
                        q_round(h, "b", (m,))
                    if not last and i == AT_QA[m]:
                        q_round(h + 1, "a", (m,))

                r = i - LAG_O
                if r % GT == 0 and exists(h, r, first) and r < TPH:
                    g = GPH * h + r // GT
                    need(act, u_ready, g + 1)
                    need(act, o_ready, GT * g)
                    act.activation(u_hi[:, :], u_ps[:, :], ACT.Copy).then_inc(u_hi_done, 1)
                if not tail:
                    par = i % 2
                    for m in range(2):
                        need(act, negmax_ready, 2 * t + m + 1)
                        need(act, attn_ready, t - 1)
                        if m == 0:
                            need(act, s1sq_ready, t - TPH + 1)
                        sums = psum1[:, i:i + 1] if m == 0 else psum2[:, par:par + 1]
                        act.activation(prob[:, par, m, :], ring[m][:, :], ACT.Exp, bias=negmax[:, par, m:m + 1],
                                       accum_out=sums).then_inc(prob_ready, 1)
                q_rounds(0)
                r = i - LAG_T
                if exists(h, r, first) and r < TPH:
                    tt = t - LAG_T
                    act.wait_ge(t_ready, tt + 1)
                    need(act, at_split, tt - 1)
                    act.activation(at32[:, r % 2, :], t_ps[:, :], ACT.Copy).then_inc(t_copied, 1)
                q_rounds(1)
                r = i - LAG_O
                if exists(h, r, first) and r < TPH:
                    tt, par = t - LAG_O, r % 2
                    act.wait_ge(o_ready, tt + 1)
                    need(act, var_ready, tt - 1)
                    need(act, ssq_ready, tt - 1)
                    act.activation(osq[:, par, :], o_ps[:, 0:DV], ACT.Square,
                                   accum_out=ssq[:, par:par + 1]).then_inc(ssq_ready, 1)

            heads(act, slot)

            def ln_squares(n):
                b = n % B
                act.wait_ge(ln_cent, n + 1)
                act.activation(sq[:, b * QT:(b + 1) * QT, :], x1[:, b * QT:(b + 1) * QT, :],
                               ACT.Square).then_inc(ln_sq, 1)

            for n in range(B):
                ln_squares(n)
            for b in range(B):
                c = slice(b * N, (b + 1) * N)
                act.wait_ge(x1t_ready, b + 1)
                act.activation(x1t[:, c], ring[b][:, :], ACT.Copy).then_inc(x1t_copied, 1)
                act.activation(xt_hi[:, c], ring[b][:, :], ACT.Copy).then_inc(x1t_hi_done, 1)
            act.wait_ge(gate_step, 2)
            act.activation(pr[:, :, :], pr[:, :, :], ACT.Exp).then_inc(gate_exp, 1)
            act.wait_ge(x1t_copied, B)
            act.wait_ge(tie_step, 7)
            act.activation(acc_t, x1t, ACT.Copy).then_inc(acc_ready, 1)

            def ffn(e, first, tail):
                if tail:
                    return
                for b in range(B):
                    for f in range(FT):
                        n = 2 * FT * e + FT * b + f
                        act.wait_ge(up_ready, n + 1)
                        need(act, g_split, n - 1)
                        act.activation(gelu[:, f % 2, :], ring[f % 2][:, :], ACT.Gelu).then_inc(gelu_ready, 1)

            experts(act, ffn)
            for b in range(B):
                act.wait_ge(back_ready, b + 1)
                act.activation(x1[:, b * QT:(b + 1) * QT, :], ring[b][:, :].rearrange("p (t d) -> p t d", d=D),
                               ACT.Copy).then_inc(back_copied, 1)
            for n in range(B, 2 * B):
                ln_squares(n)

        @block.vector
        def _(dve):
            for b in range(B):
                dve.wait_ge(x_in[b], 16)
                s = slice(b * QT, (b + 1) * QT)
                dve.tensor_copy(xk_hi[:, s, :], xres[:, s, :]).then_inc(xk_hi_done, 1)
            for b in range(B):
                c = slice(b * N, (b + 1) * N)
                dve.wait_ge(xt_hi_done, b + 1)
                dve.tensor_tensor(xt_lo[:, c], ring[b][:, :], xt_hi[:, c].bitcast(F32),
                                  ALU.subtract).then_inc(xt_split, 1)

            def m_parts(h):
                dve.wait_ge(m_ready, h + 1)
                src = ring[0][:, 0:2 * D].rearrange("p (m d) -> p m d", m=2)
                dve.tensor_scalar(m_hi[:, :, :], src, SCALE, None, ALU.mult).then_inc(m_hi_done, 1)
                dve.wait_ge(m_hi_done, h + 1)
                dve.scalar_tensor_tensor(out=m_lo[:, :, :], in0=src, scalar=SCALE, in1=m_hi[:, :, :].bitcast(F32),
                                         op0=ALU.mult, op1=ALU.subtract).then_inc(m_split, 1)

            def q_parts(h, which, maps=(0, 1)):
                for m in maps:
                    b = 1 if which == "b" else 0
                    for c in range(NCH):
                        cols = slice(c * NC, (c + 1) * NC)
                        dve.wait_ge(q_hi_done, NCH * q_index(h, which, m) + c + 1)
                        dve.tensor_tensor(q_lo[:, b, m, cols], ring[m][:, cols], q_hi[:, b, m, cols].bitcast(F32),
                                          ALU.subtract).then_inc(q_split, 1)

            m_parts(0)
            q_parts(0, "a")

            dve.wait_ge(lam_in_s, 64)
            for n in range(2):
                dve.tensor_tensor(lam_pr[:, n, :], lam_in[:, 2 * n, :], lam_in[:, 2 * n + 1, :],
                                  ALU.mult).then_inc(lam_prod, 1)
            for n in range(2):
                dve.wait_ge(lam_prod, n + 1)
                dve.reduce_sum(lam_s[:, n:n + 1], lam_pr[:, n, :], AX.X).then_inc(lam_sum, 1)
            dve.wait_ge(lam_exp, 1)
            dve.tensor_tensor(lam_s[:, 0:1], lam_s[:, 3:4], lam_s[:, 2:3], ALU.subtract).then_inc(lam_sum, 1)
            dve.wait_ge(lam_sum, 3)
            dve.tensor_scalar(lam_s[:, 1:2], lam_s[:, 0:1], -LAMBDA_INIT, None, ALU.add).then_inc(lam_sum, 1)
            dve.wait_ge(lam_sum, 4)
            dve.wait_ge(const_ready, 5)
            dve.tensor_scalar(lam_d[:, :], ident[0:H, 0:H], lam_s[:, 1:2], None, ALU.mult).then_inc(lam_diag, 1)
            dve.wait_ge(lam_ps, 1)
            dve.tensor_copy(neglam[:, :], o_ps[:, 0:H]).then_inc(lam_ready, 1)
            dve.wait_ge(rms_in, 16)
            dve.tensor_scalar(rms_c[:, :], rms_raw[:, :], (1.0 - LAMBDA_INIT) * math.sqrt(DV), None, ALU.mult).then_inc(rms_ready, 1)
            dve.wait_ge(rms_ready, 1)
            dve.wait_ge(lam_ready, 1)

            def slot(h, i, first, last, tail):
                t = TPH * h + i
                par = i % 2
                if i == 0:
                    need(dve, coef_ready, t)
                    dve.tensor_copy(neglam_h[:, :], neglam[:, bass.ds(h, 1)]).then_inc(lam_head, 1)

                def row_max(m):
                    dve.wait_ge(scores_ready, 2 * t + m + 1)
                    need(dve, prob_ready, 2 * (t - 2) + m + 1)
                    dve.tensor_reduce(negmax[:, par, m:m + 1], ring[m][:, :], axis=AX.X, op=ALU.max,
                                      negate=True).then_inc(negmax_ready, 1)

                if not tail:
                    row_max(0)
                if not tail and i == AT_WW:
                    dve.wait_ge(wp_split, h + 1)
                    need(dve, o_ready, t - AT_WW)
                    dve.tensor_copy(ww_hi[:, :], wwn_hi[:, :].bitcast(F32)).then_inc(ww_installed, 1)
                    dve.tensor_copy(ww_lo[:, :], wwn_lo[:, :].bitcast(F32)).then_inc(ww_installed, 1)
                r = i - LAG_O
                if r % GT == 0 and exists(h, r, first) and r < TPH:
                    g = GPH * h + r // GT
                    dve.wait_ge(u_hi_done, g + 1)
                    dve.tensor_tensor(u_lo[:, :], u_ps[:, :], u_hi[:, :].bitcast(F32),
                                      ALU.subtract).then_inc(u_split, 1)
                if not tail:
                    row_max(1)
                r = i - LAG_Y
                if exists(h, r, first) and r < TPH:
                    tt = t - LAG_Y
                    dve.wait_ge(fac_ready, tt + 1)
                    dst = xres[:, r % TPH, :]
                    dve.scalar_tensor_tensor(out=dst, in0=o_ps[:, DV:WWN], scalar=fac[:, r % 2:r % 2 + 1],
                                             in1=dst, op0=ALU.mult, op1=ALU.add).then_inc(y_added, 1)

                def q_lower(m):
                    if not tail and i == AT_QB[m]:
                        q_parts(h, "b", (m,))
                    if not last and i == AT_QA[m]:
                        q_parts(h + 1, "a", (m,))

                q_lower(0)
                if not last and i == AT_M:
                    m_parts(h + 1)
                if not tail and i == AT_WP:
                    dve.wait_ge(wp_ready, h + 1)
                    dve.tensor_copy(wwn_hi[:, DV:WWN], ring[0][:, 0:D]).then_inc(wp_hi_done, 1)
                    dve.wait_ge(wp_hi_done, h + 1)
                    dve.tensor_tensor(wwn_lo[:, DV:WWN], ring[0][:, 0:D], wwn_hi[:, DV:WWN].bitcast(F32),
                                      ALU.subtract).then_inc(wp_split, 1)
                if not tail:
                    dve.wait_ge(prob_ready, 2 * t + 2)
                    if i == 0:
                        dve.wait_ge(lam_head, h + 1)
                    dve.reciprocal(rs2[:, par:par + 1], psum2[:, par:par + 1]).then_inc(rs2_ready, 1)
                    dve.wait_ge(rs2_ready, t + 1)
                    dve.tensor_scalar(coef[:, par:par + 1], rs2[:, par:par + 1], psum1[:, i:i + 1],
                                      neglam_h[:, :], ALU.mult, ALU.mult).then_inc(coef_ready, 1)
                    dve.wait_ge(coef_ready, t + 1)
                    need(dve, t_ready, t - 1)
                    dve.scalar_tensor_tensor(out=attn[:, par, :], in0=prob[:, par, 1, :],
                                             scalar=coef[:, par:par + 1], in1=prob[:, par, 0, :],
                                             op0=ALU.mult, op1=ALU.add).then_inc(attn_ready, 1)
                q_lower(1)
                if not tail and i == AT_WT:
                    dve.wait_ge(wt_ready, h + 1)
                    need(dve, ww_installed, 2 * h)
                    dve.tensor_copy(wwn_hi[:, 0:DV], ring[1][:, 0:DV]).then_inc(wt_hi_done, 1)
                    dve.wait_ge(wt_hi_done, h + 1)
                    dve.tensor_tensor(wwn_lo[:, 0:DV], ring[1][:, 0:DV], wwn_hi[:, 0:DV].bitcast(F32),
                                      ALU.subtract).then_inc(wt_split, 1)
                    for m in range(2):
                        dve.tensor_scalar(wot_s[:, m, :], ring[1][:, NC + m * D:NC + (m + 1) * D],
                                          rms_c[:, m:m + 1], None, ALU.mult).then_inc(wt_split, 1)

            heads(dve, slot)

            def layer_norm(n):
                b = n % B
                s = slice(b * QT, (b + 1) * QT)
                rows_n = x1[:, s, :]

                def wide(a):
                    return a.unsqueeze(2).broadcast_to([P, QT, D])

                dve.reduce_sum(stat[:, 0, s], rows_n, AX.X).then_inc(ln_sum, 1)
                dve.wait_ge(ln_sum, n + 1)
                dve.tensor_scalar(stat[:, 3, s], stat[:, 0, s], 1.0 / D, None, ALU.mult).then_inc(ln_mean, 1)
                dve.wait_ge(ln_mean, n + 1)
                dve.tensor_tensor(rows_n, rows_n, wide(stat[:, 3, s]), ALU.subtract).then_inc(ln_cent, 1)

            def layer_norm_sums(n):
                s = slice((n % B) * QT, (n % B + 1) * QT)
                dve.wait_ge(ln_sq, n + 1)
                dve.reduce_sum(stat[:, 1, s], sq[:, s, :], AX.X).then_inc(ln_ssq, 1)

            def layer_norm_end(n):
                s = slice((n % B) * QT, (n % B + 1) * QT)
                dve.wait_ge(ln_fac, n + 1)
                dve.scalar_tensor_tensor(out=x1[:, s, :], in0=x1[:, s, :], scalar=math.sqrt(D),
                                         in1=stat[:, 2, s].unsqueeze(2).broadcast_to([P, QT, D]),
                                         op0=ALU.mult, op1=ALU.mult).then_inc(ln_done, 1)

            def norms(n0):
                for n in range(n0, n0 + B):
                    if n0:
                        dve.wait_ge(back_copied, n - n0 + 1)
                    layer_norm(n)
                for n in range(n0, n0 + B):
                    layer_norm_sums(n)
                for n in range(n0, n0 + B):
                    layer_norm_end(n)

            dve.wait_ge(y_added, H * TPH)
            norms(0)

            def w_parts(raw, hi, lo, came, hi_done, split, e):
                v = raw.rearrange("p (f c) -> p f c", c=P)
                dve.wait_ge(came, 16 * (e + 1))
                dve.tensor_copy(hi, v).then_inc(hi_done, 1)
                dve.wait_ge(hi_done, e + 1)
                dve.tensor_tensor(lo, v, hi.bitcast(F32), ALU.subtract).then_inc(split, 1)

            w_parts(w1_raw, w1_hi, w1_lo, w1_in, w1_hi_done, w1_split, 0)
            for b in range(B):
                c = slice(b * N, (b + 1) * N)
                dve.wait_ge(x1t_hi_done, b + 1)
                dve.tensor_tensor(xt_lo[:, c], ring[b][:, :], xt_hi[:, c].bitcast(F32),
                                  ALU.subtract).then_inc(x1t_split, 1)

            lg = o_ps[:, 0:QT * R].rearrange("p (t b e) -> p (t b) e", b=B, e=E)
            pv = pr[:, :, :].rearrange("p t (b e) -> p (t b) e", e=E)

            def over_e(a):
                return a.unsqueeze(2).broadcast_to([P, TPH, E])

            dve.wait_ge(gate_ready, 1)
            dve.tensor_reduce(pst[:, 0, :], lg, axis=AX.X, op=ALU.max).then_inc(gate_step, 1)
            dve.wait_ge(gate_step, 1)
            dve.tensor_tensor(pv, lg, over_e(pst[:, 0, :]), ALU.subtract).then_inc(gate_step, 1)
            dve.wait_ge(gate_exp, 1)
            dve.reduce_sum(pst[:, 1, :], pv, AX.X).then_inc(gate_step, 1)
            dve.wait_ge(gate_step, 3)
            dve.reciprocal(pst[:, 2, :], pst[:, 1, :]).then_inc(gate_step, 1)
            dve.wait_ge(gate_step, 4)
            dve.tensor_tensor(pv, pv, over_e(pst[:, 2, :]), ALU.mult).then_inc(gate_step, 1)
            dve.wait_ge(prows_ready, 1)
            dve.tensor_copy(p_rows, t_ps[0:R, :]).then_inc(prows_copied, 1)
            dve.wait_ge(rows_ready, 1)
            dve.tensor_copy(rows, t_ps[:, :]).then_inc(rows_copied, 1)

            dve.wait_ge(sel_ready, 9)
            dve.tensor_scalar(jcur[:, :], jcur[:, :], REP - 1, LB * (LEVELS - 1), ALU.bitwise_and,
                              ALU.logical_shift_left).then_inc(next_ready, 1)
            dve.wait_ge(rows_copied, 1)
            with dve.Fori(0, LEVELS) as lv:
                dve.wait_ge(next_ready, 1 + 3 * lv)
                dve.tensor_tensor(cand[:, :], base[:, :], jcur[:, :], ALU.bitwise_or).then_inc(cand_ready, 1)
                dve.wait_ge(cand_ready, lv + 1)
                dve.tensor_scalar(tie, rows, cand[:, :].bitcast(F32), None, ALU.is_ge, ALU.add,
                                  accum_out=cnt[:, :]).then_inc(cnt_ready, 1)
                dve.tensor_scalar(jcur[:, :], jcur[:, :], LB, None,
                                  ALU.logical_shift_right).then_inc(next_ready, 1)
                dve.wait_ge(cnt_ready, lv + 1)
                dve.tensor_scalar(hit[:, :], cnt[:, :], CAP - 0.5, None, ALU.is_ge).then_inc(hit_ready, 1)
                dve.wait_ge(votes_ready, lv + 1)
                dve.tensor_scalar(step[:, :], u_ps[:, 0:1], -1.0, pw[:, :], ALU.add,
                                  ALU.mult).then_inc(step_ready, 1)
                dve.wait_ge(step_ready, lv + 1)
                dve.tensor_tensor(base[:, :], base[:, :], step[:, :], ALU.bitwise_or).then_inc(next_ready, 1)
                dve.tensor_scalar(pw[:, :], pw[:, :], 1.0 / REP, None, ALU.mult).then_inc(next_ready, 1)
            dve.wait_ge(next_ready, 1 + 3 * LEVELS)
            thr = base[:, :].bitcast(F32)
            dve.tensor_scalar(tie, rows, thr, None, ALU.is_gt, ALU.add, accum_out=cnt_gt[:, :]).then_inc(tie_step, 1)
            dve.wait_ge(tie_step, 1)
            dve.tensor_scalar(free_n[:, :], cnt_gt[:, :], -1.0, float(CAP), ALU.mult, ALU.add).then_inc(tie_step, 1)
            dve.tensor_scalar(tie, rows, thr, None, ALU.is_equal).then_inc(tie_step, 1)
            dve.wait_ge(tie_step, 3)
            dve.tensor_tensor_scan(cum, tie, tie, 0.0, ALU.add, ALU.max).then_inc(tie_step, 1)
            dve.wait_ge(tie_step, 4)
            dve.scalar_tensor_tensor(out=tie, in0=cum, scalar=free_n[:, :], in1=tie, op0=ALU.is_gt,
                                     op1=ALU.mult).then_inc(tie_step, 1)
            dve.wait_ge(tie_step, 5)
            dve.scalar_tensor_tensor(out=cum, in0=rows, scalar=thr, in1=tie, op0=ALU.is_ge,
                                     op1=ALU.subtract).then_inc(tie_step, 1)
            dve.wait_ge(tie_step, 6)
            dve.tensor_tensor(rows, rows, cum, ALU.mult).then_inc(tie_step, 1)

            def g_rest(e, b):
                for f in range(FT):
                    n = 2 * FT * e + FT * b + f
                    dve.wait_ge(g_hi_done, n + 1)
                    dve.tensor_tensor(g_lo[:, b, f, :, :], gelu[:, f % 2, :].rearrange("p (c n) -> p c n", c=NCH),
                                      g_hi[:, b, f, :, :].bitcast(F32), ALU.subtract).then_inc(g_split, 1)

            def add_unit(e, b):
                u = 2 * e + b
                c = slice(b * N, (b + 1) * N)
                dve.wait_ge(w_in[b], 16 * (e + 1))
                dve.wait_ge(down_ready, u + 1)
                need(dve, acc_added, u)
                dve.tensor_tensor(prod, t_ps[:, :], weights[:, c], ALU.mult).then_inc(prod_ready, 1)
                dve.wait_ge(prod_ready, u + 1)
                if b == 0 and isinstance(e, int) and e == 0:
                    dve.wait_ge(acc_ready, 1)
                dve.tensor_tensor(acc_t[:, c], acc_t[:, c], prod, ALU.add).then_inc(acc_added, 1)

            def ffn(e, first, tail):
                if not tail:
                    g_rest(e, 0)
                if not first:
                    add_unit(e - 1, 1)
                if tail:
                    return
                w_parts(w2_raw, w2_hi, w2_lo, w2_in, w2_hi_done, w2_split, e)
                g_rest(e, 1)
                if not (isinstance(e, int) and e == E - 1):
                    dve.wait_ge(up_ready, 2 * FT * (e + 1))
                    w_parts(w1_raw, w1_hi, w1_lo, w1_in, w1_hi_done, w1_split, e + 1)
                add_unit(e, 0)

            experts(dve, ffn)
            norms(B)

        @block.tensor
        def _(pe):
            pe.wait_ge(const_ready, 5)
            for b in range(B):
                pe.wait_ge(x_in[b], 16)
                for j in range(QT):
                    last_t = pe.transpose(ring[b][:, j * P:(j + 1) * P], xres[:, b * QT + j, :], ident[:, :])
                last_t.then_inc(xt_ready, 1)

            def three(dst, a_hi, a_lo, b_hi, b_lo, start=True, stop=True):
                pe.matmul(dst, a_hi, b_hi, start=start, stop=False)
                pe.matmul(dst, a_hi, b_lo, start=False, stop=False)
                return pe.matmul(dst, a_lo, b_hi, start=False, stop=stop)

            def m_product(h):
                pe.wait_ge(qk_in, 32 * (h + 1))
                for m in range(2):
                    last_m = pe.matmul(ring[0][:, m * D:(m + 1) * D], wq_s[:, m, :], wk_s[:, m, :],
                                       start=True, stop=True)
                last_m.then_inc(m_ready, 1)

            def q_product(h, which, maps=(0, 1)):
                b = 1 if which == "b" else 0
                for m in maps:
                    for c in range(NCH):
                        cols = slice(b * N + c * NC, b * N + (c + 1) * NC)
                        three(ring[m][:, c * NC:(c + 1) * NC], m_hi[:, m, :], m_lo[:, m, :],
                              xt_hi[:, cols], xt_lo[:, cols]).then_inc(q_ready, 1)

            pe.wait_ge(xt_split, 1)
            m_product(0)
            pe.wait_ge(xt_split, 2)
            pe.wait_ge(m_split, 1)
            q_product(0, "a")
            pe.wait_ge(lam_diag, 1)
            pe.matmul(o_ps[:, 0:H], ones[0:H, :], lam_d[:, :], start=True, stop=True).then_inc(lam_ps, 1)
            pe.wait_ge(xk_split, B)
            pe.wait_ge(lam_ready, 1)

            def slot(h, i, first, last, tail):
                t = TPH * h + i
                if not tail:
                    b, qt = i // QT, i % QT
                    q = slice(qt * P, (qt + 1) * P)
                    for m in range(2):
                        need(pe, prob_ready, 2 * (t - 1) + m + 1)
                        if i == AT_M + 1 and m == 0 and not last:
                            pe.wait_ge(m_split, h + 2)
                        if i == AT_WT + 1 and m == 1:
                            pe.wait_ge(wt_split, 3 * (h + 1))
                        if i == AT_WP + 1 and m == 0:
                            pe.wait_ge(wp_split, h + 1)
                        if i == 0:
                            pe.wait_ge(q_split, NCH * (q_index(h, "a", m) + 1))
                        if i == QT:
                            pe.wait_ge(q_split, NCH * (q_index(h, "b", m) + 1))
                        for c in range(NCH):
                            if i == AT_QB[m] + 1:
                                pe.wait_ge(q_split, NCH * q_index(h, "b", m) + c + 1)
                            if i == AT_QA[m] + 1 and not last:
                                pe.wait_ge(q_split, NCH * q_index(h + 1, "a", m) + c + 1)
                            cols = slice(b * N + c * NC, b * N + (c + 1) * NC)
                            last_s = three(ring[m][:, c * NC:(c + 1) * NC], q_hi[:, b, m, q], q_lo[:, b, m, q],
                                           xt_hi[:, cols], xt_lo[:, cols])
                        last_s.then_inc(scores_ready, 1)
                r = i - LAG_T
                if exists(h, r, first) and r < TPH:
                    tt = t - LAG_T
                    pe.wait_ge(attn_ready, tt + 1)
                    need(pe, t_copied, tt)
                    for k in range(KT):
                        last_t = pe.transpose(t_ps[:, k * P:(k + 1) * P], attn[:, r % 2, k * P:(k + 1) * P],
                                              ident[:, :])
                    last_t.then_inc(t_ready, 1)
                r = i - LAG_U
                if exists(h, r, first) and r < TPH:
                    g, j = GPH * h + r // GT, r % GT
                    b, gb = (r % TPH) // QT, (r // GT) % 2
                    if j == 0:
                        pe.wait_ge(at_split, GT * (g + 1))
                        need(pe, u_split, g)
                    per = KT // GT
                    for k in range(j * per, (j + 1) * per):
                        last_u = three(u_ps[:, :], xk_hi[:, b * KT + k, :], xk_lo[:, b * KT + k, :],
                                       at_hi[:, gb, k, :], at_lo[:, gb, k, :],
                                       start=(k == 0), stop=(k == KT - 1))
                    if j == GT - 1:
                        last_u.then_inc(u_ready, 1)
                put_in = [i == AT_QB[0] and not tail, i == AT_QA[0] and not last, i == AT_WP and not tail,
                          i == AT_M and not last]
                if any(put_in):
                    pe.wait_ge(prob_ready, 2 * t + 1)
                if put_in[0]:
                    q_product(h, "b", (0,))
                if put_in[1]:
                    q_product(h + 1, "a", (0,))
                if put_in[2]:
                    for m in range(2):
                        last_w = pe.matmul(ring[0][:, 0:D], wv_s[:, m, :], wot_s[:, m, :],
                                           start=(m == 0), stop=(m == 1))
                    last_w.then_inc(wp_ready, 1)
                if put_in[3]:
                    m_product(h + 1)
                r = i - LAG_O
                if exists(h, r, first) and r < TPH:
                    tt, j = t - LAG_O, r % GT
                    g = GPH * h + r // GT
                    if j == 0:
                        pe.wait_ge(u_split, g + 1)
                    if r == 0:
                        pe.wait_ge(ww_installed, 2 * (h + 1))
                    need(pe, y_added, tt)
                    q = slice(j * P, (j + 1) * P)
                    three(o_ps[:, 0:WWN], u_hi[:, q], u_lo[:, q], ww_hi[:, :], ww_lo[:, :]).then_inc(o_ready, 1)
                put_in = [i == AT_QB[1] and not tail, i == AT_QA[1] and not last, i == AT_WT and not tail]
                if any(put_in):
                    pe.wait_ge(prob_ready, 2 * t + 2)
                if put_in[0]:
                    q_product(h, "b", (1,))
                if put_in[1]:
                    q_product(h + 1, "a", (1,))
                if put_in[2]:
                    pe.wait_ge(vo_in, 32 * (h + 1))
                    for m in range(2):
                        pe.transpose(ring[1][:, m * P:(m + 1) * P], wv_s[:, m, :], ident[:, :])
                    for m in range(2):
                        last_w = pe.transpose(ring[1][:, NC + m * P:NC + (m + 1) * P], wo_s[:, m * P:(m + 1) * P],
                                              ident[:, :])
                    last_w.then_inc(wt_ready, 1)

            heads(pe, slot)

            for b in range(B):
                pe.wait_ge(ln_done, b + 1)
                for j in range(QT):
                    last_t = pe.transpose(ring[b][:, j * P:(j + 1) * P], x1[:, b * QT + j, :], ident[:, :])
                last_t.then_inc(x1t_ready, 1)
            pe.wait_ge(gate_in, 16)
            pe.wait_ge(x1t_copied, B)
            for b in range(B):
                for j in range(QT):
                    last_g = pe.matmul(o_ps[:, j * R + b * E:j * R + (b + 1) * E],
                                       x1t[:, b * N + j * P:b * N + (j + 1) * P], gate_s[:, :],
                                       start=True, stop=True)
            last_g.then_inc(gate_ready, 1)
            pe.wait_ge(gate_step, 5)
            for j in range(QT):
                last_p = pe.transpose(t_ps[0:R, j * P:(j + 1) * P], pr[:, j, :], ident[:, :])
            last_p.then_inc(prows_ready, 1)
            pe.wait_ge(prows_copied, 1)
            pe.wait_ge(sel_ready, 9)
            for c in range(NCH):
                last_r = pe.matmul(t_ps[:, c * NC:(c + 1) * NC], sel[:, :], p_rows[:, c * NC:(c + 1) * NC],
                                   start=True, stop=True)
            last_r.then_inc(rows_ready, 1)
            with pe.Fori(0, LEVELS) as lv:
                pe.wait_ge(hit_ready, lv + 1)
                pe.matmul(u_ps[:, 0:1], grp[:, :], hit[:, :], start=True, stop=True).then_inc(votes_ready, 1)
            pe.wait_ge(x1t_split, B)

            def up(e, b):
                for f in range(FT):
                    n = 2 * FT * e + FT * b + f
                    if b == 0 and f == 0:
                        pe.wait_ge(w1_split, e + 1)
                    need(pe, gelu_ready, n - 1)
                    for c in range(NCH):
                        cols = slice(b * N + c * NC, b * N + (c + 1) * NC)
                        last_h = three(ring[f % 2][:, c * NC:(c + 1) * NC], w1_hi[:, f, :], w1_lo[:, f, :],
                                       xt_hi[:, cols], xt_lo[:, cols])
                    last_h.then_inc(up_ready, 1)

            def down(e, b):
                pe.wait_ge(w2_split, e + 1)
                need(pe, prod_ready, 2 * e + b)
                for f in range(FT):
                    pe.wait_ge(g_split, 2 * FT * e + FT * b + f + 1)
                    for c in range(NCH):
                        last_d = three(t_ps[:, c * NC:(c + 1) * NC], w2_hi[:, f, :], w2_lo[:, f, :],
                                       g_hi[:, b, f, c, :], g_lo[:, b, f, c, :],
                                       start=(f == 0), stop=(f == FT - 1))
                last_d.then_inc(down_ready, 1)

            def ffn(e, first, tail):
                if not tail:
                    up(e, 0)
                if not first:
                    down(e - 1, 1)
                if not tail:
                    up(e, 1)
                    down(e, 0)

            experts(pe, ffn)
            for b in range(B):
                pe.wait_ge(acc_added, 2 * E - 1 + b)
                for j in range(QT):
                    last_t = pe.transpose(ring[b][:, j * P:(j + 1) * P],
                                          acc_t[:, b * N + j * P:b * N + (j + 1) * P], ident[:, :])
                last_t.then_inc(back_ready, 1)


_INS = ["L0_attn_X", "L0_attn_Wq", "L0_attn_Wk", "L0_attn_Wv", "L0_attn_Wo", "L0_attn_lambda_q1",
        "L0_attn_lambda_k1", "L0_attn_lambda_q2", "L0_attn_lambda_k2", "L0_attn_rms_scale",
        "L0_ffn_gate_w", "L0_ffn_w1", "L0_ffn_w2"]


def kernel(**inputs):
    import numpy as np
    import concourse.bacc as bacc
    from concourse.bass_utils import run_bass_kernel_spmd

    nc = bacc.Bacc("TRN2", target_bir_lowering=False, num_devices=1)
    arrays, args = {}, []
    for name in _INS:
        a = np.ascontiguousarray(inputs[name])
        arrays[f"in_{name}"] = a
        args.append(nc.dram_tensor(f"in_{name}", a.shape, mybir.dt.from_np(a.dtype), kind="ExternalInput").ap())
    shape = inputs["L0_attn_X"].shape
    out = nc.dram_tensor("out_x", shape, F32, kind="ExternalOutput").ap()
    build(nc, *args, out)
    r = run_bass_kernel_spmd(nc, [arrays], core_ids=[0])
    return r.results[0]["out_x"]
```

```python
import concourse.bass as bass
from concourse import mybir
from contextlib import ExitStack
import math

F32 = mybir.dt.float32
F32R = mybir.dt.float32r
I32 = mybir.dt.int32
ALU = mybir.AluOpType
ACT = mybir.ActivationFunctionType
AX = mybir.AxisListType


def need(eng, sem, value):
    if isinstance(value, int) and value <= 0:
        return
    eng.wait_ge(sem, value)


def build(nc, X, Wq, Wk, Wv, Wo, lq1, lk1, lq2, lk2, rms_scale, gate_w, w1, w2, out):
    B, N, D = X.shape
    H, DH = lq1.shape
    DV = 2 * DH
    E = gate_w.shape[1]
    F = w1.shape[2]
    P = 128
    QT = N // P
    KT = N // P
    TPH = B * QT
    GT = 4
    GPH = TPH // GT
    NC = 512
    NCH = N // NC
    CAP = int(2.0 * N / E)
    LAMBDA_INIT = 0.8 - 0.6 * math.exp(-0.3)
    SCALE = 1.0 / math.sqrt(DH)
    EPS = 1e-5
    WWN = DV + D

    FT = F // P
    FD = FT // 2
    CT = CAP // P
    SL = B * CAP
    assert CAP % P == 0 and SL == NC
    R = B * E
    REP = P // R
    LB = REP.bit_length() - 1
    LEVELS = 30 // LB

    LAG_T = 1
    LAG_U = 6
    LAG_O = 10
    LAG_Y = 11
    AT_QB, AT_WT, AT_WP, AT_M, AT_QA = (1, 2), 4, 6, 9, (11, 13)
    AT_WW = 10

    ctx = ExitStack()
    with ctx:
        def sb(name, shape, dt=F32):
            return ctx.enter_context(nc.sbuf_tensor(name, shape, dt))

        def ps(name, shape, dt=F32):
            return ctx.enter_context(nc.psum_tensor(name, shape, dt))

        def sem(name):
            return ctx.enter_context(nc.semaphore(name))

        xres = sb("xres", [P, TPH, D])
        xk_hi = sb("xk_hi", [P, TPH, D], F32R)
        xk_lo = sb("xk_lo", [P, TPH, D], F32R)
        xt_hi = sb("xt_hi", [P, B * N], F32R)
        xt_lo = sb("xt_lo", [P, B * N], F32R)
        q_hi = sb("q_hi", [P, B, 2, N], F32R)
        q_lo = sb("q_lo", [P, B, 2, N], F32R)
        prob = sb("prob", [P, 2, 2, N])
        attn = sb("attn", [P, 2, N])
        at32 = sb("at32", [P, 2, N])
        at_hi = sb("at_hi", [P, 2, KT, NC], F32R)
        at_lo = sb("at_lo", [P, 2, KT, NC], F32R)
        u_hi = sb("u_hi", [P, NC], F32R)
        u_lo = sb("u_lo", [P, NC], F32R)
        wq_s = sb("wq_s", [P, 2, D])
        wk_s = sb("wk_s", [P, 2, D])
        wv_s = sb("wv_s", [P, 2, D])
        wo_s = sb("wo_s", [P, DV])
        wot_s = sb("wot_s", [P, 2, D])
        m_hi = sb("m_hi", [P, 2, D], F32R)
        m_lo = sb("m_lo", [P, 2, D], F32R)
        wwn_hi = sb("wwn_hi", [P, WWN], F32R)
        wwn_lo = sb("wwn_lo", [P, WWN], F32R)
        ww_hi = sb("ww_hi", [P, WWN], F32R)
        ww_lo = sb("ww_lo", [P, WWN], F32R)
        rms_c = sb("rms_c", [P, 2])
        rms_raw = sb("rms_raw", [P, 2])
        ident = sb("ident", [P, P])
        ones = sb("ones", [P, P])
        neg_half = sb("neg_half", [P, TPH])
        lam_in = sb("lam_in", [H, 4, DH])
        lam_pr = sb("lam_pr", [H, 2, DH])
        lam_s = sb("lam_s", [H, 4])
        lam_d = sb("lam_d", [H, H])
        neglam = sb("neglam", [P, H])
        neglam_h = sb("neglam_h", [P, 1])
        negmax = sb("negmax", [P, 2, 2])
        psum1 = sb("psum1", [P, TPH])
        psum2 = sb("psum2", [P, 2])
        rs2 = sb("rs2", [P, 2])
        coef = sb("coef", [P, 2])
        osq = sb("osq", [P, 2, DV])
        ssq = sb("ssq", [P, 2])
        es1 = sb("es1", [P, 2])
        s1sq = sb("s1sq", [P, TPH])
        eps_c = sb("eps_c", [P, 1])
        var_o = sb("var_o", [P, 2])
        fac = sb("fac", [P, 2])

        x1 = xres
        acc_t = prob[:, 0].rearrange("p m n -> p (m n)")
        sq = attn[:, :, :].rearrange("p a n -> p (a n)").rearrange("p (t d) -> p t d", d=D)
        x1_hi, x1_lo = xk_hi, xk_lo
        w1_raw = at32[:, 0, 0:F]
        w2_raw = at32[:, 0, F:2 * F]
        w1_hi, w2_hi = (xt_hi[:, n * F:(n + 1) * F].rearrange("p (f c) -> p f c", c=P) for n in range(2))
        w1_lo, w2_lo = (xt_lo[:, n * F:(n + 1) * F].rearrange("p (f c) -> p f c", c=P) for n in range(2))
        gat = at_hi[:, 0].rearrange("p k n -> p (k n)").rearrange("p (b t s) -> p b t s", b=B, s=CAP)
        sca = at_lo[:, 0].rearrange("p k n -> p (k n)").rearrange("p (b s t) -> p b s t", b=B, t=N)
        xs_hi, xs_lo = u_hi, u_lo
        gelu = attn[:, :, :].rearrange("p a (c n) -> p (a c) n", n=SL)
        g_hi = q_hi[:, 0].rearrange("p m (c n) -> p (m c) n", n=SL)
        g_lo = q_lo[:, 0].rearrange("p m (c n) -> p (m c) n", n=SL)
        yt = osq[:, :, :].rearrange("p a n -> p (a n)")
        y_hi = q_hi[:, 1, 0, 0:SL].rearrange("p (s d) -> p s d", d=D)
        y_lo = q_lo[:, 1, 0, 0:SL].rearrange("p (s d) -> p s d", d=D)
        prod = at32[:, 1, :].rearrange("p (a n) -> p a n", n=NC)
        weights = sb("weights", [P, B * N])
        slot_of = prob[:, 1].rearrange("p m n -> p (m n)")
        slot_row = sb("slot_row", [P, CAP])
        slot_col = sb("slot_col", [P, CT])
        slot_row_i = sb("slot_row_i", [P, CAP], I32)
        slot_col_i = sb("slot_col_i", [P, CT], I32)
        slot_tok = sb("slot_tok", [P, QT, R])
        slot_e = sb("slot_e", [P, QT, B])
        tick = sb("tick", [P, B])
        gelu_first = sb("gelu_first", [P, 1])
        gate_s = sb("gate_s", [D, E])
        stat = sb("stat", [P, 4, TPH])
        ln_eps = sb("ln_eps", [P, TPH])
        pr = sb("pr", [P, QT, R])
        pst = sb("pst", [P, 3, TPH])
        p_rows = weights[0:R, 0:N]
        rows = weights[:, N:2 * N]
        tie, cum = prob[:, 1, 0, :], prob[:, 1, 1, :]
        sel = sb("sel", [R, P])
        grp = sb("grp", [P, P])
        base = sb("base", [P, 1], I32)
        cand = sb("cand", [P, 1], I32)
        jcur = sb("jcur", [P, 1], I32)
        step = sb("step", [P, 1], I32)
        pw = sb("pw", [P, 1])
        cnt = sb("cnt", [P, 1])
        hit = sb("hit", [P, 1])
        cnt_gt = sb("cnt_gt", [P, 1])
        free_n = sb("free_n", [P, 1])
        w_dram = nc.dram_tensor("w_dram", (R, N), F32).ap()
        slot_dram = nc.dram_tensor("slot_dram", (R, N), F32).ap()

        ring = [ps("ring_a", [P, N]), ps("ring_b", [P, N])]
        t_ps = ps("t_ps", [P, N])
        u_ps = ps("u_ps", [P, NC])
        o_ps = ps("o_ps", [P, NC])

        x_in = [sem(f"x_in{b}") for b in range(B)]
        qk_in, vo_in, lam_in_s, rms_in = sem("qk_in"), sem("vo_in"), sem("lam_in_s"), sem("rms_in")
        const_ready = sem("const_ready")
        xt_ready, xt_hi_done, xt_split = sem("xt_ready"), sem("xt_hi_done"), sem("xt_split")
        xk_hi_done, xk_split = sem("xk_hi_done"), sem("xk_split")
        lam_prod, lam_sum, lam_exp, lam_diag, lam_ps = (
            sem("lam_prod"), sem("lam_sum"), sem("lam_exp"), sem("lam_diag"), sem("lam_ps"))
        lam_ready, lam_head, rms_ready = sem("lam_ready"), sem("lam_head"), sem("rms_ready")
        m_ready, m_hi_done, m_split = sem("m_ready"), sem("m_hi_done"), sem("m_split")
        q_ready, q_hi_done, q_split = sem("q_ready"), sem("q_hi_done"), sem("q_split")
        wt_ready, wt_hi_done, wt_split = sem("wt_ready"), sem("wt_hi_done"), sem("wt_split")
        wp_ready, wp_hi_done, wp_split, ww_installed = (
            sem("wp_ready"), sem("wp_hi_done"), sem("wp_split"), sem("ww_installed"))
        scores_ready, negmax_ready, prob_ready = sem("scores_ready"), sem("negmax_ready"), sem("prob_ready")
        rs2_ready, coef_ready, attn_ready = sem("rs2_ready"), sem("coef_ready"), sem("attn_ready")
        t_ready, t_copied, at_hi_done, at_split = sem("t_ready"), sem("t_copied"), sem("at_hi_done"), sem("at_split")
        u_ready, u_hi_done, u_split = sem("u_ready"), sem("u_hi_done"), sem("u_split")
        s1sq_ready = sem("s1sq_ready")
        o_ready, ssq_ready, es1_ready, var_ready, fac_ready, y_added = (
            sem("o_ready"), sem("ssq_ready"), sem("es1_ready"), sem("var_ready"), sem("fac_ready"), sem("y_added"))
        out_done = sem("out_done")
        eps_ready, ln_sum, ln_mean, ln_cent, ln_sq, ln_ssq, ln_var, ln_fac, ln_done = (
            sem("eps_ready"), sem("ln_sum"), sem("ln_mean"), sem("ln_cent"), sem("ln_sq"), sem("ln_ssq"),
            sem("ln_var"), sem("ln_fac"), sem("ln_done"))
        gate_in, x1t_ready, x1t_copied, x1_hi_done, x1_split = (
            sem("gate_in"), sem("x1t_ready"), sem("x1t_copied"), sem("x1_hi_done"), sem("x1_split"))
        gate_ready, gate_step, gate_exp, prows_ready, prows_copied, rows_ready, rows_copied = (
            sem("gate_ready"), sem("gate_step"), sem("gate_exp"), sem("prows_ready"), sem("prows_copied"),
            sem("rows_ready"), sem("rows_copied"))
        sel_ready, base_ready, cand_ready, cnt_ready, hit_ready, votes_ready, step_ready = (
            sem("sel_ready"), sem("base_ready"), sem("cand_ready"), sem("cnt_ready"), sem("hit_ready"),
            sem("votes_ready"), sem("step_ready"))
        next_ready, tie_step, w_stored, slots_stored = (
            sem("next_ready"), sem("tie_step"), sem("w_stored"), sem("slots_stored"))
        w_in, slots_in = [sem(f"w_in{b}") for b in range(B)], [sem(f"slots_in{b}") for b in range(B)]
        slot_tok_ready, slot_tok_copied, slot_e_ready, gat_ready, sca_ready = (
            sem("slot_tok_ready"), sem("slot_tok_copied"), sem("slot_e_ready"), sem("gat_ready"),
            sem("sca_ready"))
        w1_in, w2_in, w1_hi_done, w1_split, w2_hi_done, w2_split = (
            sem("w1_in"), sem("w2_in"), sem("w1_hi_done"), sem("w1_split"), sem("w2_hi_done"), sem("w2_split"))
        xs_ready, xs_copied, up_ready, gelu_ready, g_hi_done = (
            sem("xs_ready"), sem("xs_copied"), sem("up_ready"), sem("gelu_ready"), sem("g_hi_done"))
        g_split, g_split_p = sem("g_split"), sem("g_split_p")
        down_ready, yt_copied, y_ready, y_hi_done, y_split, out_ready, prod_ready, acc_added = (
            sem("down_ready"), sem("yt_copied"), sem("y_ready"), sem("y_hi_done"), sem("y_split"),
            sem("out_ready"), sem("prod_ready"), sem("acc_added"))
        back_ready, back_copied, ticked = sem("back_ready"), sem("back_copied"), sem("ticked")

        def q_index(h, which, m):
            return 4 * h + (2 if which == "b" else 0) + m

        def exists(h, r, first):
            return not (first and r < 0)

        block = ctx.enter_context(nc.Block())

        def heads(eng, slot):
            for i in range(TPH):
                slot(0, i, True, False, False)
            with eng.Fori(1, H - 1) as h:
                for i in range(TPH):
                    slot(h, i, False, False, False)
            for i in range(TPH):
                slot(H - 1, i, False, True, False)
            for i in range(TPH, TPH + LAG_Y):
                slot(H - 1, i, False, True, True)

        def experts(eng, step_of):
            step_of(0, True, False)
            step_of(1, False, False)
            with eng.Fori(2, E - 2) as e:
                step_of(e, False, False)
            step_of(E - 2, False, False)
            step_of(E - 1, False, False)
            step_of(E, False, True)

        def is_at(e, n):
            return isinstance(e, int) and e == n

        @block.sync
        def _(sp):
            for b in range(B):
                sp.dma_start(xres[:, b * QT:(b + 1) * QT, :],
                             X[b].rearrange("(t p) d -> p t d", p=P)).then_inc(x_in[b], 16)
            wq_v = Wq.rearrange("(h m e) d -> h e m d", m=2, e=P)
            wk_v = Wk.rearrange("(h m e) d -> h e m d", m=2, e=P)
            wv_v = Wv.rearrange("(h m e) d -> h e m d", m=2, e=P)
            wo_v = Wo.rearrange("d (h e) -> h d e", e=DV)

            def load_qk(h):
                sp.dma_start(wq_s[:, :, :], wq_v[bass.ds(h, 1)].rearrange("a e m d -> (a e) m d")).then_inc(qk_in, 16)
                sp.dma_start(wk_s[:, :, :], wk_v[bass.ds(h, 1)].rearrange("a e m d -> (a e) m d")).then_inc(qk_in, 16)

            def load_vo(h):
                sp.dma_start(wv_s[:, :, :], wv_v[bass.ds(h, 1)].rearrange("a e m d -> (a e) m d")).then_inc(vo_in, 16)
                sp.dma_start(wo_s[:, :], wo_v[bass.ds(h, 1)].rearrange("a d e -> (a d) e")).then_inc(vo_in, 16)

            load_qk(0)
            load_vo(0)
            for n, v in enumerate((lq1, lk1, lq2, lk2)):
                sp.dma_start(lam_in[:, n, :], v).then_inc(lam_in_s, 16)
            with nc.allow_non_contiguous_dma(reason="256 numbers, once"):
                sp.dma_start(rms_raw[:, :], rms_scale.rearrange("(m e) -> e m", e=P)).then_inc(rms_in, 16)
            with sp.Fori(1, H) as h:
                sp.wait_ge(m_ready, h)
                load_qk(h)
                sp.wait_ge(wp_ready, h)
                load_vo(h)
            sp.dma_start(gate_s[:, :], gate_w).then_inc(gate_in, 16)
            w2_v = w2.rearrange("e (f p) c -> e p f c", p=P)

            def load_w1(e):
                sp.dma_start(w1_raw, w1[bass.ds(e, 1)].rearrange("a c f -> (a c) f")).then_inc(w1_in, 16)

            def load_w2(e):
                sp.dma_start(w2_raw.rearrange("p (f c) -> p f c", f=FT),
                             w2_v[bass.ds(e, 1)].rearrange("a p f c -> (a p) f c")).then_inc(w2_in, 16)

            def load_row(dst, rows_d, e, b, came):
                src = rows_d.rearrange("(b e) n -> b e n", b=B)[b][bass.ds(e, 1), :]
                sp.dma_start(dst[:, b * N:(b + 1) * N],
                             src.rearrange("a n -> (a n)").partition_broadcast(P)).then_inc(came[b], 16)

            sp.wait_ge(at_split, H * TPH)
            load_w1(0)
            load_w2(0)
            sp.wait_ge(rows_copied, 1)
            sp.dma_start(w_dram, rows[0:P:REP, :]).then_inc(w_stored, 16)
            sp.wait_ge(tie_step, 8)
            sp.dma_start(slot_dram, cum[0:P:REP, :]).then_inc(slots_stored, 16)
            sp.wait_ge(slots_stored, 16)
            sp.wait_ge(slot_tok_ready, 1)
            for b in range(B):
                load_row(slot_of, slot_dram, 0, b, slots_in)
            sp.wait_ge(w_stored, 16)
            for b in range(B):
                load_row(weights, w_dram, 0, b, w_in)

            def next_w1(e):
                sp.wait_ge(w1_split, e)
                load_w1(e)

            def next_w2(e):
                sp.wait_ge(w2_split, e)
                load_w2(e)

            def next_slots(e):
                for b in range(B):
                    sp.wait_ge(sca_ready, 2 * (e - 1) + b + 1)
                    load_row(slot_of, slot_dram, e, b, slots_in)

            def next_weights(e):
                for b in range(B):
                    sp.wait_ge(prod_ready, NCH * (B * (e - 1) + b + 1))
                    load_row(weights, w_dram, e, b, w_in)

            for e in (1, 2):
                next_w1(e)
                next_w2(e)
            next_slots(1)
            with sp.Fori(1, E - 2) as e:
                next_w1(e + 2)
                next_weights(e)
                next_w2(e + 2)
                next_slots(e + 1)
            next_weights(E - 2)
            next_slots(E - 1)
            next_weights(E - 1)
            for b in range(B):
                sp.wait_ge(ln_done, B + b + 1)
                sp.dma_start(out[b].rearrange("(t p) d -> p t d", p=P),
                             x1[:, b * QT:(b + 1) * QT, :]).then_inc(out_done, 16)
            sp.wait_ge(out_done, 16 * B)

        @block.gpsimd
        def _(pool):
            pool.memset(ident[:, :], 0.0).then_inc(const_ready, 1)
            pool.memset(ones[:, :], 1.0).then_inc(const_ready, 1)
            pool.memset(neg_half[:, :], -0.5).then_inc(const_ready, 1)
            pool.memset(eps_c[:, :], EPS * DV).then_inc(const_ready, 1)
            pool.wait_ge(const_ready, 4)
            pool.affine_select(out=ident[:, :], in_=ident[:, :], compare_op=ALU.not_equal, fill=1.0, base=0,
                               pattern=[[-1, P]], channel_multiplier=1).then_inc(const_ready, 1)
            for b in range(B):
                pool.wait_ge(xk_hi_done, b + 1)
                s = slice(b * QT, (b + 1) * QT)
                pool.tensor_tensor(xk_lo[:, s, :], xres[:, s, :], xk_hi[:, s, :].bitcast(F32),
                                   ALU.subtract).then_inc(xk_split, 1)

            def slot(h, i, first, last, tail):
                t = TPH * h + i
                r = i - LAG_O
                if exists(h, r, first) and r < TPH:
                    tt, par = t - LAG_O, r % 2
                    pool.wait_ge(s1sq_ready, tt + 1)
                    need(pool, var_ready, tt - 1)
                    pool.tensor_tensor(es1[:, par:par + 1], s1sq[:, r % TPH:r % TPH + 1], eps_c[:, 0:1],
                                       ALU.mult).then_inc(es1_ready, 1)
                    pool.wait_ge(es1_ready, tt + 1)
                    pool.wait_ge(ssq_ready, tt + 1)
                    pool.tensor_tensor(var_o[:, par:par + 1], ssq[:, par:par + 1], es1[:, par:par + 1],
                                       ALU.add).then_inc(var_ready, 1)
                    need(pool, y_added, tt - 1)
                    pool.wait_ge(var_ready, tt + 1)
                    pool.tensor_tensor(fac[:, par:par + 1], var_o[:, par:par + 1], neg_half[:, 0:1],
                                       ALU.pow).then_inc(fac_ready, 1)
                r = i - LAG_T
                if exists(h, r, first) and r < TPH:
                    tt, par, g = t - LAG_T, r % 2, (r // GT) % 2
                    need(pool, t_copied, tt + 1)
                    gabs = GPH * h + r // GT
                    if not (first and r // GT < 2):
                        pool.wait_ge(u_ready, gabs - 1)
                    s1 = psum1[:, r % TPH:r % TPH + 1]
                    pool.tensor_tensor(s1sq[:, r % TPH:r % TPH + 1], s1, s1, ALU.mult).then_inc(s1sq_ready, 1)
                    c = slice((r % GT) * P, (r % GT + 1) * P)
                    src = at32[:, par, :].rearrange("p (k q) -> p k q", q=P)
                    pool.tensor_scalar(at_hi[:, g, :, c], src, 1.0, 0.0, ALU.mult, ALU.add).then_inc(at_hi_done, 1)
                    pool.wait_ge(at_hi_done, tt + 1)
                    pool.tensor_tensor(at_lo[:, g, :, c], src, at_hi[:, g, :, c].bitcast(F32),
                                       ALU.subtract).then_inc(at_split, 1)

            heads(pool, slot)

            def ln_factors(n):
                c = slice((n % B) * QT, (n % B + 1) * QT)
                pool.wait_ge(ln_ssq, n + 1)
                pool.tensor_tensor(stat[:, 1, c], stat[:, 1, c], ln_eps[:, c], ALU.add).then_inc(ln_var, 1)
                pool.wait_ge(ln_var, n + 1)
                pool.tensor_tensor(stat[:, 2, c], stat[:, 1, c], neg_half[:, c], ALU.pow).then_inc(ln_fac, 1)

            pool.memset(ln_eps[:, :], EPS * D).then_inc(eps_ready, 1)
            pool.wait_ge(eps_ready, 1)
            pool.memset(sel[:, :], 1.0).then_inc(sel_ready, 1)
            pool.memset(grp[:, :], 1.0).then_inc(sel_ready, 1)
            pool.memset(base[:, :], 0).then_inc(sel_ready, 1)
            pool.memset(pw[:, :], float(2 ** (LB * (LEVELS - 1)))).then_inc(sel_ready, 1)
            pool.iota(jcur[:, :], pattern=[[0, 1]], base=0, channel_multiplier=1).then_inc(sel_ready, 1)
            for n, (buf, pat, mult) in enumerate((
                    (sel[:, :], [[1, P]], -REP),
                    (grp[:, :].rearrange("p (g j) -> p g j", j=REP), [[-REP, R], [0, REP]], 1))):
                pool.wait_ge(sel_ready, 5 + 2 * n)
                pool.affine_select(out=buf, in_=buf, compare_op=ALU.is_ge, fill=0.0, base=0, pattern=pat,
                                   channel_multiplier=mult).then_inc(sel_ready, 1)
                pool.wait_ge(sel_ready, 6 + 2 * n)
                pool.affine_select(out=buf, in_=buf, compare_op=ALU.is_ge, fill=0.0, base=REP - 1,
                                   pattern=[[-a, c] for a, c in pat], channel_multiplier=-mult).then_inc(sel_ready, 1)
            pool.iota(slot_row_i[:, :], pattern=[[1, CAP]], base=1, channel_multiplier=0).then_inc(sel_ready, 1)
            pool.iota(slot_col_i[:, :], pattern=[[P, CT]], base=1, channel_multiplier=1).then_inc(sel_ready, 1)
            for n in range(B):
                ln_factors(n)
            for b in range(B):
                s = slice(b * QT, (b + 1) * QT)
                pool.wait_ge(x1_hi_done, b + 1)
                pool.tensor_tensor(x1_lo[:, s, :], x1[:, s, :], x1_hi[:, s, :].bitcast(F32),
                                   ALU.subtract).then_inc(x1_split, 1)

            def w_lower(raw, hi, lo, hi_done, split, e):
                pool.wait_ge(hi_done, e + 1)
                pool.tensor_tensor(lo, raw.rearrange("p (f c) -> p f c", c=P), hi.bitcast(F32),
                                  ALU.subtract).then_inc(split, 1)

            w_lower(w1_raw, w1_hi, w1_lo, w1_hi_done, w1_split, 0)
            w_lower(w2_raw, w2_hi, w2_lo, w2_hi_done, w2_split, 0)

            def add_out(e):
                for k in range(B * NCH):
                    n = B * NCH * e + k
                    pool.wait_ge(prod_ready, n + 1)
                    c = slice(k * NC, (k + 1) * NC)
                    pool.tensor_tensor(acc_t[:, c], acc_t[:, c], prod[:, k % 2, :], ALU.add).then_inc(acc_added, 1)

            def ffn(e, first, tail):
                if not tail:
                    for f in range(FD, FT):
                        pool.wait_ge(g_hi_done, FT * e + f + 1)
                        pool.tensor_tensor(g_lo[:, f, :], gelu[:, f, :], g_hi[:, f, :].bitcast(F32),
                                           ALU.subtract).then_inc(g_split_p, 1)
                    if not is_at(e, E - 1):
                        w_lower(w1_raw, w1_hi, w1_lo, w1_hi_done, w1_split, e + 1)
                if not first:
                    add_out(e - 1)
                if not tail and not is_at(e, E - 1):
                    w_lower(w2_raw, w2_hi, w2_lo, w2_hi_done, w2_split, e + 1)

            experts(pool, ffn)
            for n in range(B, 2 * B):
                ln_factors(n)

        @block.scalar
        def _(act):
            for b in range(B):
                act.wait_ge(xt_ready, b + 1)
                act.activation(xt_hi[:, b * N:(b + 1) * N], ring[b][:, :], ACT.Copy).then_inc(xt_hi_done, 1)
            def q_round(h, which, maps=(0, 1)):
                for m in maps:
                    b = 1 if which == "b" else 0
                    for c in range(NCH):
                        cols = slice(c * NC, (c + 1) * NC)
                        act.wait_ge(q_ready, NCH * q_index(h, which, m) + c + 1)
                        act.activation(q_hi[:, b, m, cols], ring[m][:, cols], ACT.Copy).then_inc(q_hi_done, 1)

            q_round(0, "a")
            act.wait_ge(lam_sum, 2)
            act.activation(lam_s[:, 2:4], lam_s[:, 0:2], ACT.Exp).then_inc(lam_exp, 1)

            def slot(h, i, first, last, tail):
                t = TPH * h + i

                def q_rounds(m):
                    if not tail and i == AT_QB[m]:
                        q_round(h, "b", (m,))
                    if not last and i == AT_QA[m]:
                        q_round(h + 1, "a", (m,))

                r = i - LAG_O
                if r % GT == 0 and exists(h, r, first) and r < TPH:
                    g = GPH * h + r // GT
                    need(act, u_ready, g + 1)
                    need(act, o_ready, GT * g)
                    act.activation(u_hi[:, :], u_ps[:, :], ACT.Copy).then_inc(u_hi_done, 1)
                if not tail:
                    par = i % 2
                    for m in range(2):
                        need(act, negmax_ready, 2 * t + m + 1)
                        need(act, attn_ready, t - 1)
                        if m == 0:
                            need(act, s1sq_ready, t - TPH + 1)
                        sums = psum1[:, i:i + 1] if m == 0 else psum2[:, par:par + 1]
                        act.activation(prob[:, par, m, :], ring[m][:, :], ACT.Exp, bias=negmax[:, par, m:m + 1],
                                       accum_out=sums).then_inc(prob_ready, 1)
                q_rounds(0)
                r = i - LAG_T
                if exists(h, r, first) and r < TPH:
                    tt = t - LAG_T
                    act.wait_ge(t_ready, tt + 1)
                    need(act, at_split, tt - 1)
                    act.activation(at32[:, r % 2, :], t_ps[:, :], ACT.Copy).then_inc(t_copied, 1)
                q_rounds(1)
                r = i - LAG_O
                if exists(h, r, first) and r < TPH:
                    tt, par = t - LAG_O, r % 2
                    act.wait_ge(o_ready, tt + 1)
                    need(act, var_ready, tt - 1)
                    need(act, ssq_ready, tt - 1)
                    act.activation(osq[:, par, :], o_ps[:, 0:DV], ACT.Square,
                                   accum_out=ssq[:, par:par + 1]).then_inc(ssq_ready, 1)

            heads(act, slot)

            def ln_squares(n):
                b = n % B
                act.wait_ge(ln_cent, n + 1)
                act.activation(sq[:, b * QT:(b + 1) * QT, :], x1[:, b * QT:(b + 1) * QT, :],
                               ACT.Square).then_inc(ln_sq, 1)

            for n in range(B):
                ln_squares(n)
            for b in range(B):
                act.wait_ge(x1t_ready, b + 1)
                act.activation(acc_t[:, b * N:(b + 1) * N], ring[b][:, :], ACT.Copy).then_inc(x1t_copied, 1)
            for b in range(B):
                s = slice(b * QT, (b + 1) * QT)
                act.activation(x1_hi[:, s, :], x1[:, s, :], ACT.Copy).then_inc(x1_hi_done, 1)
            act.wait_ge(gate_step, 2)
            act.activation(pr[:, :, :], pr[:, :, :], ACT.Exp).then_inc(gate_exp, 1)
            act.activation(gelu_first[:, :], eps_c[:, :], ACT.Gelu).then_inc(ticked, 1)

            def w_round(raw, hi, came, used, hi_done, e):
                act.wait_ge(came, 16 * (e + 1))
                if not is_at(e, 0):
                    act.wait_ge(*used)
                act.activation(hi, raw.rearrange("p (f c) -> p f c", c=P), ACT.Copy).then_inc(hi_done, 1)

            def xs_copy(e):
                for part, (dst, src) in enumerate(((xs_hi, u_ps), (xs_lo, o_ps))):
                    act.wait_ge(xs_ready, 2 * e + part + 1)
                    if part == 0 and not is_at(e, 0):
                        act.wait_ge(up_ready, FT * e)
                    act.activation(dst[:, :], src[:, :], ACT.Copy).then_inc(xs_copied, 1)

            w_round(w1_raw, w1_hi, w1_in, None, w1_hi_done, 0)
            w_round(w2_raw, w2_hi, w2_in, None, w2_hi_done, 0)
            xs_copy(0)

            def ffn(e, first, tail):
                if tail:
                    return
                for f in range(FT):
                    n = FT * e + f
                    act.wait_ge(up_ready, n + 1)
                    if f < FD:
                        need(act, g_split, FD * (e - 1) + f + 1)
                    else:
                        need(act, g_split_p, (FT - FD) * (e - 1) + f - FD + 1)
                    act.activation(gelu[:, f, :], ring[0][:, (f % 2) * SL:(f % 2 + 1) * SL],
                                   ACT.Gelu).then_inc(gelu_ready, 1)
                    act.wait_ge(gelu_ready, n + 1)
                    need(act, down_ready, e)
                    act.activation(g_hi[:, f, :], gelu[:, f, :], ACT.Copy).then_inc(g_hi_done, 1)
                if not is_at(e, E - 1):
                    w_round(w1_raw, w1_hi, w1_in, (up_ready, FT * (e + 1)), w1_hi_done, e + 1)
                    xs_copy(e + 1)
                act.wait_ge(down_ready, e + 1)
                need(act, y_ready, e)
                act.activation(yt, t_ps[:, 0:SL], ACT.Copy).then_inc(yt_copied, 1)
                if not is_at(e, E - 1):
                    w_round(w2_raw, w2_hi, w2_in, (down_ready, e + 1), w2_hi_done, e + 1)
                act.wait_ge(y_ready, e + 1)
                need(act, out_ready, B * NCH * e)
                act.activation(y_hi, t_ps[:, NC:NC + SL].rearrange("p (s d) -> p s d", d=D),
                               ACT.Copy).then_inc(y_hi_done, 1)

            experts(act, ffn)
            for b in range(B):
                act.wait_ge(back_ready, b + 1)
                act.activation(x1[:, b * QT:(b + 1) * QT, :], ring[b][:, :].rearrange("p (t d) -> p t d", d=D),
                               ACT.Copy).then_inc(back_copied, 1)
            for n in range(B, 2 * B):
                ln_squares(n)

        @block.vector
        def _(dve):
            for b in range(B):
                dve.wait_ge(x_in[b], 16)
                s = slice(b * QT, (b + 1) * QT)
                dve.tensor_copy(xk_hi[:, s, :], xres[:, s, :]).then_inc(xk_hi_done, 1)
            for b in range(B):
                c = slice(b * N, (b + 1) * N)
                dve.wait_ge(xt_hi_done, b + 1)
                dve.tensor_tensor(xt_lo[:, c], ring[b][:, :], xt_hi[:, c].bitcast(F32),
                                  ALU.subtract).then_inc(xt_split, 1)

            def m_parts(h):
                dve.wait_ge(m_ready, h + 1)
                src = ring[0][:, 0:2 * D].rearrange("p (m d) -> p m d", m=2)
                dve.tensor_scalar(m_hi[:, :, :], src, SCALE, None, ALU.mult).then_inc(m_hi_done, 1)
                dve.wait_ge(m_hi_done, h + 1)
                dve.scalar_tensor_tensor(out=m_lo[:, :, :], in0=src, scalar=SCALE, in1=m_hi[:, :, :].bitcast(F32),
                                         op0=ALU.mult, op1=ALU.subtract).then_inc(m_split, 1)

            def q_parts(h, which, maps=(0, 1)):
                for m in maps:
                    b = 1 if which == "b" else 0
                    for c in range(NCH):
                        cols = slice(c * NC, (c + 1) * NC)
                        dve.wait_ge(q_hi_done, NCH * q_index(h, which, m) + c + 1)
                        dve.tensor_tensor(q_lo[:, b, m, cols], ring[m][:, cols], q_hi[:, b, m, cols].bitcast(F32),
                                          ALU.subtract).then_inc(q_split, 1)

            m_parts(0)
            q_parts(0, "a")

            dve.wait_ge(lam_in_s, 64)
            for n in range(2):
                dve.tensor_tensor(lam_pr[:, n, :], lam_in[:, 2 * n, :], lam_in[:, 2 * n + 1, :],
                                  ALU.mult).then_inc(lam_prod, 1)
            for n in range(2):
                dve.wait_ge(lam_prod, n + 1)
                dve.reduce_sum(lam_s[:, n:n + 1], lam_pr[:, n, :], AX.X).then_inc(lam_sum, 1)
            dve.wait_ge(lam_exp, 1)
            dve.tensor_tensor(lam_s[:, 0:1], lam_s[:, 3:4], lam_s[:, 2:3], ALU.subtract).then_inc(lam_sum, 1)
            dve.wait_ge(lam_sum, 3)
            dve.tensor_scalar(lam_s[:, 1:2], lam_s[:, 0:1], -LAMBDA_INIT, None, ALU.add).then_inc(lam_sum, 1)
            dve.wait_ge(lam_sum, 4)
            dve.wait_ge(const_ready, 5)
            dve.tensor_scalar(lam_d[:, :], ident[0:H, 0:H], lam_s[:, 1:2], None, ALU.mult).then_inc(lam_diag, 1)
            dve.wait_ge(lam_ps, 1)
            dve.tensor_copy(neglam[:, :], o_ps[:, 0:H]).then_inc(lam_ready, 1)
            dve.wait_ge(rms_in, 16)
            dve.tensor_scalar(rms_c[:, :], rms_raw[:, :], (1.0 - LAMBDA_INIT) * math.sqrt(DV), None, ALU.mult).then_inc(rms_ready, 1)
            dve.wait_ge(rms_ready, 1)
            dve.wait_ge(lam_ready, 1)

            def slot(h, i, first, last, tail):
                t = TPH * h + i
                par = i % 2
                if i == 0:
                    need(dve, coef_ready, t)
                    dve.tensor_copy(neglam_h[:, :], neglam[:, bass.ds(h, 1)]).then_inc(lam_head, 1)

                def row_max(m):
                    dve.wait_ge(scores_ready, 2 * t + m + 1)
                    need(dve, prob_ready, 2 * (t - 2) + m + 1)
                    dve.tensor_reduce(negmax[:, par, m:m + 1], ring[m][:, :], axis=AX.X, op=ALU.max,
                                      negate=True).then_inc(negmax_ready, 1)

                if not tail:
                    row_max(0)
                if not tail and i == AT_WW:
                    dve.wait_ge(wp_split, h + 1)
                    need(dve, o_ready, t - AT_WW)
                    dve.tensor_copy(ww_hi[:, :], wwn_hi[:, :].bitcast(F32)).then_inc(ww_installed, 1)
                    dve.tensor_copy(ww_lo[:, :], wwn_lo[:, :].bitcast(F32)).then_inc(ww_installed, 1)
                r = i - LAG_O
                if r % GT == 0 and exists(h, r, first) and r < TPH:
                    g = GPH * h + r // GT
                    dve.wait_ge(u_hi_done, g + 1)
                    dve.tensor_tensor(u_lo[:, :], u_ps[:, :], u_hi[:, :].bitcast(F32),
                                      ALU.subtract).then_inc(u_split, 1)
                if not tail:
                    row_max(1)
                r = i - LAG_Y
                if exists(h, r, first) and r < TPH:
                    tt = t - LAG_Y
                    dve.wait_ge(fac_ready, tt + 1)
                    dst = xres[:, r % TPH, :]
                    dve.scalar_tensor_tensor(out=dst, in0=o_ps[:, DV:WWN], scalar=fac[:, r % 2:r % 2 + 1],
                                             in1=dst, op0=ALU.mult, op1=ALU.add).then_inc(y_added, 1)

                def q_lower(m):
                    if not tail and i == AT_QB[m]:
                        q_parts(h, "b", (m,))
                    if not last and i == AT_QA[m]:
                        q_parts(h + 1, "a", (m,))

                q_lower(0)
                if not last and i == AT_M:
                    m_parts(h + 1)
                if not tail and i == AT_WP:
                    dve.wait_ge(wp_ready, h + 1)
                    dve.tensor_copy(wwn_hi[:, DV:WWN], ring[0][:, 0:D]).then_inc(wp_hi_done, 1)
                    dve.wait_ge(wp_hi_done, h + 1)
                    dve.tensor_tensor(wwn_lo[:, DV:WWN], ring[0][:, 0:D], wwn_hi[:, DV:WWN].bitcast(F32),
                                      ALU.subtract).then_inc(wp_split, 1)
                if not tail:
                    dve.wait_ge(prob_ready, 2 * t + 2)
                    if i == 0:
                        dve.wait_ge(lam_head, h + 1)
                    dve.reciprocal(rs2[:, par:par + 1], psum2[:, par:par + 1]).then_inc(rs2_ready, 1)
                    dve.wait_ge(rs2_ready, t + 1)
                    dve.tensor_scalar(coef[:, par:par + 1], rs2[:, par:par + 1], psum1[:, i:i + 1],
                                      neglam_h[:, :], ALU.mult, ALU.mult).then_inc(coef_ready, 1)
                    dve.wait_ge(coef_ready, t + 1)
                    need(dve, t_ready, t - 1)
                    dve.scalar_tensor_tensor(out=attn[:, par, :], in0=prob[:, par, 1, :],
                                             scalar=coef[:, par:par + 1], in1=prob[:, par, 0, :],
                                             op0=ALU.mult, op1=ALU.add).then_inc(attn_ready, 1)
                q_lower(1)
                if not tail and i == AT_WT:
                    dve.wait_ge(wt_ready, h + 1)
                    need(dve, ww_installed, 2 * h)
                    dve.tensor_copy(wwn_hi[:, 0:DV], ring[1][:, 0:DV]).then_inc(wt_hi_done, 1)
                    dve.wait_ge(wt_hi_done, h + 1)
                    dve.tensor_tensor(wwn_lo[:, 0:DV], ring[1][:, 0:DV], wwn_hi[:, 0:DV].bitcast(F32),
                                      ALU.subtract).then_inc(wt_split, 1)
                    for m in range(2):
                        dve.tensor_scalar(wot_s[:, m, :], ring[1][:, NC + m * D:NC + (m + 1) * D],
                                          rms_c[:, m:m + 1], None, ALU.mult).then_inc(wt_split, 1)

            heads(dve, slot)

            def layer_norm(n):
                b = n % B
                s = slice(b * QT, (b + 1) * QT)
                rows_n = x1[:, s, :]

                def wide(a):
                    return a.unsqueeze(2).broadcast_to([P, QT, D])

                dve.reduce_sum(stat[:, 0, s], rows_n, AX.X).then_inc(ln_sum, 1)
                dve.wait_ge(ln_sum, n + 1)
                dve.tensor_scalar(stat[:, 3, s], stat[:, 0, s], 1.0 / D, None, ALU.mult).then_inc(ln_mean, 1)
                dve.wait_ge(ln_mean, n + 1)
                dve.tensor_tensor(rows_n, rows_n, wide(stat[:, 3, s]), ALU.subtract).then_inc(ln_cent, 1)

            def layer_norm_sums(n):
                s = slice((n % B) * QT, (n % B + 1) * QT)
                dve.wait_ge(ln_sq, n + 1)
                dve.reduce_sum(stat[:, 1, s], sq[:, s, :], AX.X).then_inc(ln_ssq, 1)

            def layer_norm_end(n):
                s = slice((n % B) * QT, (n % B + 1) * QT)
                dve.wait_ge(ln_fac, n + 1)
                dve.scalar_tensor_tensor(out=x1[:, s, :], in0=x1[:, s, :], scalar=math.sqrt(D),
                                         in1=stat[:, 2, s].unsqueeze(2).broadcast_to([P, QT, D]),
                                         op0=ALU.mult, op1=ALU.mult).then_inc(ln_done, 1)

            def norms(n0):
                for n in range(n0, n0 + B):
                    if n0:
                        dve.wait_ge(back_copied, n - n0 + 1)
                    layer_norm(n)
                for n in range(n0, n0 + B):
                    layer_norm_sums(n)
                for n in range(n0, n0 + B):
                    layer_norm_end(n)

            dve.wait_ge(y_added, H * TPH)
            norms(0)

            lg = o_ps[:, 0:QT * R].rearrange("p (t b e) -> p (t b) e", b=B, e=E)
            pv = pr[:, :, :].rearrange("p t (b e) -> p (t b) e", e=E)

            def over_e(a):
                return a.unsqueeze(2).broadcast_to([P, TPH, E])

            dve.wait_ge(gate_ready, 1)
            dve.tensor_reduce(pst[:, 0, :], lg, axis=AX.X, op=ALU.max).then_inc(gate_step, 1)
            dve.wait_ge(gate_step, 1)
            dve.tensor_tensor(pv, lg, over_e(pst[:, 0, :]), ALU.subtract).then_inc(gate_step, 1)
            dve.wait_ge(gate_exp, 1)
            dve.reduce_sum(pst[:, 1, :], pv, AX.X).then_inc(gate_step, 1)
            dve.wait_ge(gate_step, 3)
            dve.reciprocal(pst[:, 2, :], pst[:, 1, :]).then_inc(gate_step, 1)
            dve.wait_ge(gate_step, 4)
            dve.tensor_tensor(pv, pv, over_e(pst[:, 2, :]), ALU.mult).then_inc(gate_step, 1)
            dve.wait_ge(prows_ready, 1)
            dve.tensor_copy(p_rows, t_ps[0:R, :]).then_inc(prows_copied, 1)
            dve.wait_ge(rows_ready, 1)
            dve.tensor_copy(rows, t_ps[:, :]).then_inc(rows_copied, 1)

            dve.wait_ge(sel_ready, 11)
            dve.tensor_copy(slot_row[:, :], slot_row_i[:, :]).then_inc(slot_tok_copied, 1)
            dve.tensor_copy(slot_col[:, :], slot_col_i[:, :]).then_inc(slot_tok_copied, 1)
            dve.tensor_scalar(jcur[:, :], jcur[:, :], REP - 1, LB * (LEVELS - 1), ALU.bitwise_and,
                              ALU.logical_shift_left).then_inc(next_ready, 1)
            dve.wait_ge(rows_copied, 1)
            with dve.Fori(0, LEVELS) as lv:
                dve.wait_ge(next_ready, 1 + 3 * lv)
                dve.tensor_tensor(cand[:, :], base[:, :], jcur[:, :], ALU.bitwise_or).then_inc(cand_ready, 1)
                dve.wait_ge(cand_ready, lv + 1)
                dve.tensor_scalar(tie, rows, cand[:, :].bitcast(F32), None, ALU.is_ge, ALU.add,
                                  accum_out=cnt[:, :]).then_inc(cnt_ready, 1)
                dve.tensor_scalar(jcur[:, :], jcur[:, :], LB, None,
                                  ALU.logical_shift_right).then_inc(next_ready, 1)
                dve.wait_ge(cnt_ready, lv + 1)
                dve.tensor_scalar(hit[:, :], cnt[:, :], CAP - 0.5, None, ALU.is_ge).then_inc(hit_ready, 1)
                dve.wait_ge(votes_ready, lv + 1)
                dve.tensor_scalar(step[:, :], u_ps[:, 0:1], -1.0, pw[:, :], ALU.add,
                                  ALU.mult).then_inc(step_ready, 1)
                dve.wait_ge(step_ready, lv + 1)
                dve.tensor_tensor(base[:, :], base[:, :], step[:, :], ALU.bitwise_or).then_inc(next_ready, 1)
                dve.tensor_scalar(pw[:, :], pw[:, :], 1.0 / REP, None, ALU.mult).then_inc(next_ready, 1)
            dve.wait_ge(next_ready, 1 + 3 * LEVELS)
            thr = base[:, :].bitcast(F32)
            dve.tensor_scalar(tie, rows, thr, None, ALU.is_gt, ALU.add, accum_out=cnt_gt[:, :]).then_inc(tie_step, 1)
            dve.wait_ge(tie_step, 1)
            dve.tensor_scalar(free_n[:, :], cnt_gt[:, :], -1.0, float(CAP), ALU.mult, ALU.add).then_inc(tie_step, 1)
            dve.tensor_scalar(tie, rows, thr, None, ALU.is_equal).then_inc(tie_step, 1)
            dve.wait_ge(tie_step, 3)
            dve.tensor_tensor_scan(cum, tie, tie, 0.0, ALU.add, ALU.max).then_inc(tie_step, 1)
            dve.wait_ge(tie_step, 4)
            dve.scalar_tensor_tensor(out=tie, in0=cum, scalar=free_n[:, :], in1=tie, op0=ALU.is_gt,
                                     op1=ALU.mult).then_inc(tie_step, 1)
            dve.wait_ge(tie_step, 5)
            dve.scalar_tensor_tensor(out=tie, in0=rows, scalar=thr, in1=tie, op0=ALU.is_ge,
                                     op1=ALU.subtract).then_inc(tie_step, 1)
            dve.wait_ge(tie_step, 6)
            dve.tensor_tensor_scan(cum, tie, tie, 0.0, ALU.add, ALU.max).then_inc(tie_step, 1)
            dve.wait_ge(tie_step, 7)
            dve.tensor_tensor(cum, cum, tie, ALU.mult).then_inc(tie_step, 1)

            def gather_ones(e):
                if not is_at(e, 0):
                    dve.wait_ge(xs_ready, 2 * e)
                need(dve, gat_ready, 2 * e)
                dve.tensor_copy(slot_e[:, :, :].rearrange("p t (b a) -> p t b a", a=1),
                                slot_tok[:, :, :].rearrange("p t (b e) -> p t b e", e=E)[:, :, :, bass.ds(e, 1)]
                                ).then_inc(slot_e_ready, 1)
                dve.wait_ge(slot_e_ready, e + 1)
                for b in range(B):
                    for j in range(QT):
                        last_c = dve.tensor_scalar(gat[:, b, j, :], slot_row[:, :], slot_e[:, j, b:b + 1], None,
                                                   ALU.is_equal)
                    last_c.then_inc(gat_ready, 1)

            def scatter_ones(e):
                for b in range(B):
                    dve.wait_ge(slots_in[b], 16 * (e + 1))
                    need(dve, out_ready, B * NCH * (e - 1) + NCH * (b + 1))
                    dve.tensor_copy(tick[:, b:b + 1], slot_col[:, 0:1]).then_inc(ticked, 1)
                    for j in range(CT):
                        last_c = dve.tensor_scalar(sca[:, b, j, :], slot_of[:, b * N:(b + 1) * N],
                                                   slot_col[:, j:j + 1], None, ALU.is_equal)
                    last_c.then_inc(sca_ready, 1)

            def weighted(e):
                for k in range(B * NCH):
                    n, b = B * NCH * e + k, k // NCH
                    if k % NCH == 0:
                        dve.wait_ge(w_in[b], 16 * (e + 1))
                    dve.wait_ge(out_ready, n + 1)
                    need(dve, acc_added, n - 1)
                    dve.tensor_tensor(prod[:, k % 2, :], ring[1][:, (k % 2) * NC:(k % 2 + 1) * NC],
                                      weights[:, k * NC:(k + 1) * NC], ALU.mult).then_inc(prod_ready, 1)

            dve.wait_ge(slot_tok_ready, 1)
            dve.tensor_copy(slot_tok[:, :, :], t_ps[:, :].rearrange("p (t r j) -> p t r j", r=R, j=REP)[:, :, :, 0]
                            ).then_inc(slot_tok_copied, 1)
            dve.wait_ge(slot_tok_copied, 3)
            gather_ones(0)
            gather_ones(1)

            def ffn(e, first, tail):
                if not tail:
                    for f in range(FD):
                        dve.wait_ge(g_hi_done, FT * e + f + 1)
                        dve.tensor_tensor(g_lo[:, f, :], gelu[:, f, :], g_hi[:, f, :].bitcast(F32),
                                          ALU.subtract).then_inc(g_split, 1)
                    if not is_at(e, E - 2) and not is_at(e, E - 1):
                        gather_ones(e + 2)
                if not first:
                    weighted(e - 1)
                if not tail:
                    dve.wait_ge(y_hi_done, e + 1)
                    dve.tensor_tensor(y_lo, t_ps[:, NC:NC + SL].rearrange("p (s d) -> p s d", d=D),
                                      y_hi.bitcast(F32), ALU.subtract).then_inc(y_split, 1)
                    scatter_ones(e)

            experts(dve, ffn)
            norms(B)

        @block.tensor
        def _(pe):
            pe.wait_ge(const_ready, 5)
            for b in range(B):
                pe.wait_ge(x_in[b], 16)
                for j in range(QT):
                    last_t = pe.transpose(ring[b][:, j * P:(j + 1) * P], xres[:, b * QT + j, :], ident[:, :])
                last_t.then_inc(xt_ready, 1)

            def three(dst, a_hi, a_lo, b_hi, b_lo, start=True, stop=True):
                pe.matmul(dst, a_hi, b_hi, start=start, stop=False)
                pe.matmul(dst, a_hi, b_lo, start=False, stop=False)
                return pe.matmul(dst, a_lo, b_hi, start=False, stop=stop)

            def m_product(h):
                pe.wait_ge(qk_in, 32 * (h + 1))
                for m in range(2):
                    last_m = pe.matmul(ring[0][:, m * D:(m + 1) * D], wq_s[:, m, :], wk_s[:, m, :],
                                       start=True, stop=True)
                last_m.then_inc(m_ready, 1)

            def q_product(h, which, maps=(0, 1)):
                b = 1 if which == "b" else 0
                for m in maps:
                    for c in range(NCH):
                        cols = slice(b * N + c * NC, b * N + (c + 1) * NC)
                        three(ring[m][:, c * NC:(c + 1) * NC], m_hi[:, m, :], m_lo[:, m, :],
                              xt_hi[:, cols], xt_lo[:, cols]).then_inc(q_ready, 1)

            pe.wait_ge(xt_split, 1)
            m_product(0)
            pe.wait_ge(xt_split, 2)
            pe.wait_ge(m_split, 1)
            q_product(0, "a")
            pe.wait_ge(lam_diag, 1)
            pe.matmul(o_ps[:, 0:H], ones[0:H, :], lam_d[:, :], start=True, stop=True).then_inc(lam_ps, 1)
            pe.wait_ge(xk_split, B)
            pe.wait_ge(lam_ready, 1)

            def slot(h, i, first, last, tail):
                t = TPH * h + i
                if not tail:
                    b, qt = i // QT, i % QT
                    q = slice(qt * P, (qt + 1) * P)
                    for m in range(2):
                        need(pe, prob_ready, 2 * (t - 1) + m + 1)
                        if i == AT_M + 1 and m == 0 and not last:
                            pe.wait_ge(m_split, h + 2)
                        if i == AT_WT + 1 and m == 1:
                            pe.wait_ge(wt_split, 3 * (h + 1))
                        if i == AT_WP + 1 and m == 0:
                            pe.wait_ge(wp_split, h + 1)
                        if i == 0:
                            pe.wait_ge(q_split, NCH * (q_index(h, "a", m) + 1))
                        if i == QT:
                            pe.wait_ge(q_split, NCH * (q_index(h, "b", m) + 1))
                        for c in range(NCH):
                            if i == AT_QB[m] + 1:
                                pe.wait_ge(q_split, NCH * q_index(h, "b", m) + c + 1)
                            if i == AT_QA[m] + 1 and not last:
                                pe.wait_ge(q_split, NCH * q_index(h + 1, "a", m) + c + 1)
                            cols = slice(b * N + c * NC, b * N + (c + 1) * NC)
                            last_s = three(ring[m][:, c * NC:(c + 1) * NC], q_hi[:, b, m, q], q_lo[:, b, m, q],
                                           xt_hi[:, cols], xt_lo[:, cols])
                        last_s.then_inc(scores_ready, 1)
                r = i - LAG_T
                if exists(h, r, first) and r < TPH:
                    tt = t - LAG_T
                    pe.wait_ge(attn_ready, tt + 1)
                    need(pe, t_copied, tt)
                    for k in range(KT):
                        last_t = pe.transpose(t_ps[:, k * P:(k + 1) * P], attn[:, r % 2, k * P:(k + 1) * P],
                                              ident[:, :])
                    last_t.then_inc(t_ready, 1)
                r = i - LAG_U
                if exists(h, r, first) and r < TPH:
                    g, j = GPH * h + r // GT, r % GT
                    b, gb = (r % TPH) // QT, (r // GT) % 2
                    if j == 0:
                        pe.wait_ge(at_split, GT * (g + 1))
                        need(pe, u_split, g)
                    per = KT // GT
                    for k in range(j * per, (j + 1) * per):
                        last_u = three(u_ps[:, :], xk_hi[:, b * KT + k, :], xk_lo[:, b * KT + k, :],
                                       at_hi[:, gb, k, :], at_lo[:, gb, k, :],
                                       start=(k == 0), stop=(k == KT - 1))
                    if j == GT - 1:
                        last_u.then_inc(u_ready, 1)
                put_in = [i == AT_QB[0] and not tail, i == AT_QA[0] and not last, i == AT_WP and not tail,
                          i == AT_M and not last]
                if any(put_in):
                    pe.wait_ge(prob_ready, 2 * t + 1)
                if put_in[0]:
                    q_product(h, "b", (0,))
                if put_in[1]:
                    q_product(h + 1, "a", (0,))
                if put_in[2]:
                    for m in range(2):
                        last_w = pe.matmul(ring[0][:, 0:D], wv_s[:, m, :], wot_s[:, m, :],
                                           start=(m == 0), stop=(m == 1))
                    last_w.then_inc(wp_ready, 1)
                if put_in[3]:
                    m_product(h + 1)
                r = i - LAG_O
                if exists(h, r, first) and r < TPH:
                    tt, j = t - LAG_O, r % GT
                    g = GPH * h + r // GT
                    if j == 0:
                        pe.wait_ge(u_split, g + 1)
                    if r == 0:
                        pe.wait_ge(ww_installed, 2 * (h + 1))
                    need(pe, y_added, tt)
                    q = slice(j * P, (j + 1) * P)
                    three(o_ps[:, 0:WWN], u_hi[:, q], u_lo[:, q], ww_hi[:, :], ww_lo[:, :]).then_inc(o_ready, 1)
                put_in = [i == AT_QB[1] and not tail, i == AT_QA[1] and not last, i == AT_WT and not tail]
                if any(put_in):
                    pe.wait_ge(prob_ready, 2 * t + 2)
                if put_in[0]:
                    q_product(h, "b", (1,))
                if put_in[1]:
                    q_product(h + 1, "a", (1,))
                if put_in[2]:
                    pe.wait_ge(vo_in, 32 * (h + 1))
                    for m in range(2):
                        pe.transpose(ring[1][:, m * P:(m + 1) * P], wv_s[:, m, :], ident[:, :])
                    for m in range(2):
                        last_w = pe.transpose(ring[1][:, NC + m * P:NC + (m + 1) * P], wo_s[:, m * P:(m + 1) * P],
                                              ident[:, :])
                    last_w.then_inc(wt_ready, 1)

            heads(pe, slot)

            for b in range(B):
                pe.wait_ge(ln_done, b + 1)
                for j in range(QT):
                    last_t = pe.transpose(ring[b][:, j * P:(j + 1) * P], x1[:, b * QT + j, :], ident[:, :])
                last_t.then_inc(x1t_ready, 1)
            pe.wait_ge(gate_in, 16)
            pe.wait_ge(x1t_copied, B)
            for b in range(B):
                for j in range(QT):
                    last_g = pe.matmul(o_ps[:, j * R + b * E:j * R + (b + 1) * E],
                                       acc_t[:, b * N + j * P:b * N + (j + 1) * P], gate_s[:, :],
                                       start=True, stop=True)
            last_g.then_inc(gate_ready, 1)
            pe.wait_ge(gate_step, 5)
            for j in range(QT):
                last_p = pe.transpose(t_ps[0:R, j * P:(j + 1) * P], pr[:, j, :], ident[:, :])
            last_p.then_inc(prows_ready, 1)
            pe.wait_ge(prows_copied, 1)
            pe.wait_ge(sel_ready, 9)
            for c in range(NCH):
                last_r = pe.matmul(t_ps[:, c * NC:(c + 1) * NC], sel[:, :], p_rows[:, c * NC:(c + 1) * NC],
                                   start=True, stop=True)
            last_r.then_inc(rows_ready, 1)
            with pe.Fori(0, LEVELS) as lv:
                pe.wait_ge(hit_ready, lv + 1)
                pe.matmul(u_ps[:, 0:1], grp[:, :], hit[:, :], start=True, stop=True).then_inc(votes_ready, 1)
            pe.wait_ge(tie_step, 8)
            for j in range(QT):
                last_t = pe.transpose(t_ps[:, j * P:(j + 1) * P], cum[:, j * P:(j + 1) * P], ident[:, :])
            last_t.then_inc(slot_tok_ready, 1)

            def gather(e):
                for part, (dst, src) in enumerate(((u_ps, x1_hi), (o_ps, x1_lo))):
                    for b in range(B):
                        if part == 0:
                            pe.wait_ge(gat_ready, 2 * e + b + 1)
                        if b == 0 and not is_at(e, 0):
                            pe.wait_ge(xs_copied, 2 * e)
                        for j in range(QT):
                            last_x = pe.matmul(dst[:, b * CAP:(b + 1) * CAP], src[:, b * QT + j, :],
                                               gat[:, b, j, :], start=(j == 0), stop=(j == QT - 1))
                    last_x.then_inc(xs_ready, 1)

            def up(e):
                pe.wait_ge(w1_split, e + 1)
                pe.wait_ge(xs_copied, 2 * (e + 1))
                for f in range(FT):
                    need(pe, gelu_ready, FT * e + f - 1)
                    three(ring[0][:, (f % 2) * SL:(f % 2 + 1) * SL], w1_hi[:, f, :], w1_lo[:, f, :],
                          xs_hi[:, :], xs_lo[:, :]).then_inc(up_ready, 1)

            def down(e):
                pe.wait_ge(w2_split, e + 1)
                need(pe, yt_copied, e)
                for f in range(FT):
                    if f < FD:
                        pe.wait_ge(g_split, FD * e + f + 1)
                    else:
                        pe.wait_ge(g_split_p, (FT - FD) * e + f - FD + 1)
                    last_d = three(t_ps[:, 0:SL], w2_hi[:, f, :], w2_lo[:, f, :], g_hi[:, f, :], g_lo[:, f, :],
                                   start=(f == 0), stop=(f == FT - 1))
                last_d.then_inc(down_ready, 1)

            def y_slots(e):
                pe.wait_ge(yt_copied, e + 1)
                need(pe, y_split, e)
                for j in range(B * CT):
                    last_t = pe.transpose(t_ps[:, NC + j * P:NC + (j + 1) * P], yt[:, j * P:(j + 1) * P],
                                          ident[:, :])
                last_t.then_inc(y_ready, 1)

            def scatter(e):
                pe.wait_ge(y_split, e + 1)
                for k in range(B * NCH):
                    n, b, c = B * NCH * e + k, k // NCH, k % NCH
                    if c == 0:
                        pe.wait_ge(sca_ready, 2 * e + b + 1)
                    need(pe, prod_ready, n - 1)
                    for j in range(CT):
                        for part, y_part in enumerate((y_hi, y_lo)):
                            last_o = pe.matmul(ring[1][:, (k % 2) * NC:(k % 2 + 1) * NC], y_part[:, b * CT + j, :],
                                               sca[:, b, j, c * NC:(c + 1) * NC],
                                               start=(j == 0 and part == 0), stop=(j == CT - 1 and part == 1))
                    last_o.then_inc(out_ready, 1)

            pe.wait_ge(x1_split, B)
            gather(0)

            def ffn(e, first, tail):
                if not tail:
                    up(e)
                    if not is_at(e, E - 1):
                        gather(e + 1)
                    down(e)
                if not first:
                    scatter(e - 1)
                if not tail:
                    y_slots(e)

            experts(pe, ffn)
            for b in range(B):
                pe.wait_ge(acc_added, B * NCH * (E - 1) + NCH * (b + 1))
                for j in range(QT):
                    last_t = pe.transpose(ring[b][:, j * P:(j + 1) * P],
                                          acc_t[:, b * N + j * P:b * N + (j + 1) * P], ident[:, :])
                last_t.then_inc(back_ready, 1)


_INS = ["L0_attn_X", "L0_attn_Wq", "L0_attn_Wk", "L0_attn_Wv", "L0_attn_Wo", "L0_attn_lambda_q1",
        "L0_attn_lambda_k1", "L0_attn_lambda_q2", "L0_attn_lambda_k2", "L0_attn_rms_scale",
        "L0_ffn_gate_w", "L0_ffn_w1", "L0_ffn_w2"]


def kernel(**inputs):
    import numpy as np
    import concourse.bacc as bacc
    from concourse.bass_utils import run_bass_kernel_spmd

    nc = bacc.Bacc("TRN2", target_bir_lowering=False, num_devices=1)
    arrays, args = {}, []
    for name in _INS:
        a = np.ascontiguousarray(inputs[name])
        arrays[f"in_{name}"] = a
        args.append(nc.dram_tensor(f"in_{name}", a.shape, mybir.dt.from_np(a.dtype), kind="ExternalInput").ap())
    shape = inputs["L0_attn_X"].shape
    out = nc.dram_tensor("out_x", shape, F32, kind="ExternalOutput").ap()
    build(nc, *args, out)
    r = run_bass_kernel_spmd(nc, [arrays], core_ids=[0])
    return r.results[0]["out_x"]
```

```python
import concourse.bass as bass
from concourse import mybir
from contextlib import ExitStack
import math

F32 = mybir.dt.float32
F32R = mybir.dt.float32r
I32 = mybir.dt.int32
ALU = mybir.AluOpType
ACT = mybir.ActivationFunctionType
AX = mybir.AxisListType


def need(eng, sem, value):
    if isinstance(value, int) and value <= 0:
        return
    eng.wait_ge(sem, value)


def build(nc, X, Wq, Wk, Wv, Wo, lq1, lk1, lq2, lk2, rms_scale, gate_w, w1, w2, out):
    B, N, D = X.shape
    H, DH = lq1.shape
    DV = 2 * DH
    E = gate_w.shape[1]
    F = w1.shape[2]
    P = 128
    QT = N // P
    KT = N // P
    TPH = B * QT
    GT = 4
    GPH = TPH // GT
    NC = 512
    NCH = N // NC
    PER = KT // GT
    CAP = int(2.0 * N / E)
    LAMBDA_INIT = 0.8 - 0.6 * math.exp(-0.3)
    SCALE = 1.0 / math.sqrt(DH)
    EPS = 1e-5
    WWN = DV + D

    FT = F // P
    FD = FT // 2
    GAT_SPLIT = 12
    CT = CAP // P
    SL = B * CAP
    assert CAP % P == 0 and SL == NC and FT == 4
    R = B * E
    REP = P // R
    LB = REP.bit_length() - 1
    LEVELS = 30 // LB
    LEVELS_PT = 5
    assert LEVELS * LB == 30 and LEVELS % LEVELS_PT == 0

    LAG_T = 1
    LAG_U = 6
    LAG_O = 10
    LAG_Y = 11
    AT_QB, AT_WT, AT_WP, AT_M, AT_QA = (1, 2), 4, 6, 9, (11, 13)
    AT_LN = (18, 19, 20, 21, 22)
    AT_WW = 10

    ctx = ExitStack()
    with ctx:
        def sb(name, shape, dt=F32):
            return ctx.enter_context(nc.sbuf_tensor(name, shape, dt))

        def ps(name, shape, dt=F32):
            return ctx.enter_context(nc.psum_tensor(name, shape, dt))

        def sem(name):
            return ctx.enter_context(nc.semaphore(name))

        xres = sb("xres", [P, TPH, D])
        xk_hi = sb("xk_hi", [P, TPH, D], F32R)
        xk_lo = sb("xk_lo", [P, TPH, D], F32R)
        xt_hi = sb("xt_hi", [P, B * N], F32R)
        xt_lo = sb("xt_lo", [P, B * N], F32R)
        q_hi = sb("q_hi", [P, B, 2, N], F32R)
        q_lo = sb("q_lo", [P, B, 2, N], F32R)
        prob = sb("prob", [P, 2, 2, N])
        attn = sb("attn", [P, 2, N])
        at32 = sb("at32", [P, 2, N])
        at_hi = sb("at_hi", [P, 2, KT, NC], F32R)
        at_lo = sb("at_lo", [P, 2, KT, NC], F32R)
        u_hi = sb("u_hi", [P, NC], F32R)
        u_lo = sb("u_lo", [P, NC], F32R)
        wq_s = sb("wq_s", [P, 2, D])
        wk_s = sb("wk_s", [P, 2, D])
        wv_s = sb("wv_s", [P, 2, D])
        wo_s = sb("wo_s", [P, DV])
        wot_s = sb("wot_s", [P, 2, D])
        m_hi = sb("m_hi", [P, 2, D], F32R)
        m_lo = sb("m_lo", [P, 2, D], F32R)
        wwn_hi = sb("wwn_hi", [P, WWN], F32R)
        wwn_lo = sb("wwn_lo", [P, WWN], F32R)
        ww_hi = sb("ww_hi", [P, WWN], F32R)
        ww_lo = sb("ww_lo", [P, WWN], F32R)
        rms_c = sb("rms_c", [P, 2])
        rms_raw = sb("rms_raw", [P, 2])
        ident = sb("ident", [P, P])
        ones = sb("ones", [P, P])
        neg_half = sb("neg_half", [P, TPH])
        lam_in = sb("lam_in", [H, 4, DH])
        lam_pr = sb("lam_pr", [H, 2, DH])
        lam_s = sb("lam_s", [H, 4])
        lam_d = sb("lam_d", [H, H])
        neglam = sb("neglam", [P, H])
        neglam_h = sb("neglam_h", [P, 1])
        negmax = sb("negmax", [P, 2, 2])
        psum1 = sb("psum1", [P, TPH])
        psum2 = sb("psum2", [P, 2])
        rs2 = sb("rs2", [P, 2])
        coef = sb("coef", [P, 2])
        osq = sb("osq", [P, 2, DV])
        ssq = sb("ssq", [P, 2])
        es1 = sb("es1", [P, 2])
        s1sq = sb("s1sq", [P, TPH])
        eps_c = sb("eps_c", [P, 1])
        var_o = sb("var_o", [P, 2])
        fac = sb("fac", [P, 2])

        x1 = xres
        acc_t = prob[:, 0].rearrange("p m n -> p (m n)")
        sq = attn[:, :, :].rearrange("p a n -> p (a n)").rearrange("p (t d) -> p t d", d=D)
        x1_hi, x1_lo = xk_hi, xk_lo
        w1_raw = at32[:, 0, 0:F]
        w2_raw = at32[:, 0, F:2 * F]
        w1_hi, w2_hi = (xt_hi[:, n * F:(n + 1) * F].rearrange("p (f c) -> p f c", c=P) for n in range(2))
        w1_lo, w2_lo = (xt_lo[:, n * F:(n + 1) * F].rearrange("p (f c) -> p f c", c=P) for n in range(2))
        gat = at_hi[:, 0].rearrange("p k n -> p (k n)").rearrange("p (b t s) -> p b t s", b=B, s=CAP)
        sca = at_lo[:, 0].rearrange("p k n -> p (k n)").rearrange("p (b s t) -> p b s t", b=B, t=N)
        sca_last = at_lo[:, 1].rearrange("p k n -> p (k n)").rearrange("p (b s t) -> p b s t", b=B, t=N)
        xs_hi, xs_lo = u_hi, u_lo
        gelu = attn[:, :, :].rearrange("p a (c n) -> p (a c) n", n=SL)
        g_hi = q_hi[:, 0].rearrange("p m (c n) -> p (m c) n", n=SL)
        g_lo = q_lo[:, 0].rearrange("p m (c n) -> p (m c) n", n=SL)
        yt = osq[:, :, :].rearrange("p a n -> p (a n)")
        y_hi = q_hi[:, 1, 0, 0:SL].rearrange("p (s d) -> p s d", d=D)
        y_lo = q_lo[:, 1, 0, 0:SL].rearrange("p (s d) -> p s d", d=D)
        y_hi_last = q_hi[:, 1, 1, 0:SL].rearrange("p (s d) -> p s d", d=D)
        y_lo_last = q_lo[:, 1, 1, 0:SL].rearrange("p (s d) -> p s d", d=D)
        prod = at32[:, 1, :].rearrange("p (a n) -> p a n", n=NC)
        weights = sb("weights", [P, B * N])
        slot_of = prob[:, 1].rearrange("p m n -> p (m n)")
        slot_row = sb("slot_row", [P, CAP])
        slot_col = sb("slot_col", [P, CT])
        slot_row_i = sb("slot_row_i", [P, CAP], I32)
        slot_col_i = sb("slot_col_i", [P, CT], I32)
        slot_tok = sb("slot_tok", [P, QT, R])
        slot_e = sb("slot_e", [P, QT, B])
        tick = sb("tick", [P, B])
        gelu_first = sb("gelu_first", [P, 1])
        gate_s = sb("gate_s", [D, E])
        stat = sb("stat", [P, 4, TPH])
        ln_eps = sb("ln_eps", [P, TPH])
        pr = sb("pr", [P, QT, R])
        pst = sb("pst", [P, 3, TPH])
        pr_rep = weights[:, 0:N]
        rows = weights[:, N:2 * N]
        tie, cum = prob[:, 1, 0, :], prob[:, 1, 1, :]
        grp = sb("grp", [P, P])
        base = sb("base", [P, 1], I32)
        base_j = sb("base_j", [P, 1], I32)
        cand = sb("cand", [P, 1], I32)
        jcur = sb("jcur", [P, 1], I32)
        step = sb("step", [P, 1], I32)
        pw = sb("pw", [P, 1])
        cnt = sb("cnt", [P, 1])
        hit = sb("hit", [P, 1])
        cnt_gt = sb("cnt_gt", [P, 1])
        free_n = sb("free_n", [P, 1])
        w_dram = nc.dram_tensor("w_dram", (R, N), F32).ap()
        slot_dram = nc.dram_tensor("slot_dram", (R, N), F32).ap()

        ring = [ps("ring_a", [P, N]), ps("ring_b", [P, N])]
        t_ps = ps("t_ps", [P, N])
        u_ps = ps("u_ps", [P, NC])
        o_ps = ps("o_ps", [P, NC])

        x1t_ps = [t_ps, ring[1]]

        x_in = [sem(f"x_in{b}") for b in range(B)]
        qk_in, vo_in, lam_in_s, rms_in = sem("qk_in"), sem("vo_in"), sem("lam_in_s"), sem("rms_in")
        const_ready = sem("const_ready")
        xt_ready, xt_hi_done, xt_split = sem("xt_ready"), sem("xt_hi_done"), sem("xt_split")
        xk_hi_done, xk_split = sem("xk_hi_done"), sem("xk_split")
        lam_prod, lam_sum, lam_exp, lam_diag, lam_ps = (
            sem("lam_prod"), sem("lam_sum"), sem("lam_exp"), sem("lam_diag"), sem("lam_ps"))
        lam_ready, lam_head, rms_ready = sem("lam_ready"), sem("lam_head"), sem("rms_ready")
        m_ready, m_hi_done, m_split = sem("m_ready"), sem("m_hi_done"), sem("m_split")
        q_ready, q_hi_done, q_split = sem("q_ready"), sem("q_hi_done"), sem("q_split")
        wt_ready, wt_hi_done, wt_split = sem("wt_ready"), sem("wt_hi_done"), sem("wt_split")
        wp_ready, wp_hi_done, wp_split, ww_installed = (
            sem("wp_ready"), sem("wp_hi_done"), sem("wp_split"), sem("ww_installed"))
        scores_ready, negmax_ready, prob_ready = sem("scores_ready"), sem("negmax_ready"), sem("prob_ready")
        rs2_ready, coef_ready, attn_ready = sem("rs2_ready"), sem("coef_ready"), sem("attn_ready")
        t_ready, t_copied, at_hi_done, at_split = sem("t_ready"), sem("t_copied"), sem("at_hi_done"), sem("at_split")
        u_ready, u_hi_done, u_split = sem("u_ready"), sem("u_hi_done"), sem("u_split")
        s1sq_ready, s1sq_last, last_hi_done = sem("s1sq_ready"), sem("s1sq_last"), sem("last_hi_done")
        o_ready, ssq_ready, es1_ready, var_ready, fac_ready, y_added = (
            sem("o_ready"), sem("ssq_ready"), sem("es1_ready"), sem("var_ready"), sem("fac_ready"), sem("y_added"))
        out_done = sem("out_done")
        eps_ready, ln_sum, ln_mean, ln_cent, ln_sq, ln_ssq, ln_var, ln_fac, ln_done = (
            sem("eps_ready"), sem("ln_sum"), sem("ln_mean"), sem("ln_cent"), sem("ln_sq"), sem("ln_ssq"),
            sem("ln_var"), sem("ln_fac"), sem("ln_done"))
        gate_in, x1t_ready, x1t_copied, x1_hi_done, x1_split = (
            sem("gate_in"), sem("x1t_ready"), sem("x1t_copied"), sem("x1_hi_done"), sem("x1_split"))
        gate_ready, gate_step, gate_exp, rows_ready, rows_copied = (
            sem("gate_ready"), sem("gate_step"), sem("gate_exp"),
            sem("rows_ready"), sem("rows_copied"))
        topk_const, cand_ready, cnt_ready, hit_ready, votes_ready, step_ready = (
            sem("topk_const"), sem("cand_ready"), sem("cnt_ready"), sem("hit_ready"),
            sem("votes_ready"), sem("step_ready"))
        next_ready, tie_step, w_stored, slots_stored = (
            sem("next_ready"), sem("tie_step"), sem("w_stored"), sem("slots_stored"))
        w_in, slots_in = [sem(f"w_in{b}") for b in range(B)], [sem(f"slots_in{b}") for b in range(B)]
        slot_tok_ready, slot_tok_copied, slot_e_ready, gat_ready, sca_ready = (
            sem("slot_tok_ready"), sem("slot_tok_copied"), sem("slot_e_ready"), sem("gat_ready"),
            sem("sca_ready"))
        w1_in, w2_in, w1_hi_done, w1_split, w2_hi_done, w2_split = (
            sem("w1_in"), sem("w2_in"), sem("w1_hi_done"), sem("w1_split"), sem("w2_hi_done"), sem("w2_split"))
        xs_ready, xs_copied, up_ready, gelu_ready, g_hi_done = (
            sem("xs_ready"), sem("xs_copied"), sem("up_ready"), sem("gelu_ready"), sem("g_hi_done"))
        g_split, g_split_p = sem("g_split"), sem("g_split_p")
        down_ready, yt_copied, y_ready, y_hi_done, y_split, out_ready, prod_ready, acc_added, acc_added_dve = (
            sem("down_ready"), sem("yt_copied"), sem("y_ready"), sem("y_hi_done"), sem("y_split"),
            sem("out_ready"), sem("prod_ready"), sem("acc_added"), sem("acc_added_dve"))
        back_ready, ticked = sem("back_ready"), sem("ticked")

        def q_index(h, which, m):
            return 4 * h + (2 if which == "b" else 0) + m

        def o_bank(r, last):
            if not last or r < TPH - LAG_O:
                return o_ps[:, :]
            return ring[r % 4 // 2][:, (r % 2) * NC:(r % 2 + 1) * NC]

        def up_bank(f):
            return t_ps[:, 0:SL] if f == 2 else ring[0][:, (f % 3) * SL:(f % 3 + 1) * SL]

        def exists(h, r, first):
            return not (first and r < 0)

        block = ctx.enter_context(nc.Block())

        def heads(eng, slot):
            for i in range(TPH):
                slot(0, i, True, False, False)
            with eng.Fori(1, H - 1) as h:
                for i in range(TPH):
                    slot(h, i, False, False, False)
            for i in range(TPH):
                slot(H - 1, i, False, True, False)
            for i in range(TPH, TPH + LAG_Y):
                slot(H - 1, i, False, True, True)

        def experts(eng, step_of):
            step_of(0, True, False)
            step_of(1, False, False)
            with eng.Fori(2, E - 2) as e:
                step_of(e, False, False)
            step_of(E - 2, False, False)
            step_of(E - 1, False, False)
            step_of(E, False, True)

        def sca_of(e):
            return sca_last if is_at(e, E - 1) else sca

        def y_parts(e):
            return (y_hi_last, y_lo_last) if is_at(e, E - 1) else (y_hi, y_lo)

        def is_at(e, n):
            return isinstance(e, int) and e == n

        @block.sync
        def _(sp):
            for b in range(B):
                sp.dma_start(xres[:, b * QT:(b + 1) * QT, :],
                             X[b].rearrange("(t p) d -> p t d", p=P)).then_inc(x_in[b], 16)
            wq_v = Wq.rearrange("(h m e) d -> h e m d", m=2, e=P)
            wk_v = Wk.rearrange("(h m e) d -> h e m d", m=2, e=P)
            wv_v = Wv.rearrange("(h m e) d -> h e m d", m=2, e=P)
            wo_v = Wo.rearrange("d (h e) -> h d e", e=DV)

            def load_qk(h):
                sp.dma_start(wq_s[:, :, :], wq_v[bass.ds(h, 1)].rearrange("a e m d -> (a e) m d")).then_inc(qk_in, 16)
                sp.dma_start(wk_s[:, :, :], wk_v[bass.ds(h, 1)].rearrange("a e m d -> (a e) m d")).then_inc(qk_in, 16)

            def load_vo(h):
                sp.dma_start(wv_s[:, :, :], wv_v[bass.ds(h, 1)].rearrange("a e m d -> (a e) m d")).then_inc(vo_in, 16)
                sp.dma_start(wo_s[:, :], wo_v[bass.ds(h, 1)].rearrange("a d e -> (a d) e")).then_inc(vo_in, 16)

            load_qk(0)
            load_vo(0)
            for n, v in enumerate((lq1, lk1, lq2, lk2)):
                sp.dma_start(lam_in[:, n, :], v).then_inc(lam_in_s, 16)
            with nc.allow_non_contiguous_dma(reason="256 numbers, once"):
                sp.dma_start(rms_raw[:, :], rms_scale.rearrange("(m e) -> e m", e=P)).then_inc(rms_in, 16)
            with sp.Fori(1, H) as h:
                sp.wait_ge(m_ready, h)
                load_qk(h)
                sp.wait_ge(wp_ready, h)
                load_vo(h)
            sp.dma_start(gate_s[:, :], gate_w).then_inc(gate_in, 16)
            w2_v = w2.rearrange("e (f p) c -> e p f c", p=P)

            def load_w1(e):
                sp.dma_start(w1_raw, w1[bass.ds(e, 1)].rearrange("a c f -> (a c) f")).then_inc(w1_in, 16)

            def load_w2(e):
                sp.dma_start(w2_raw.rearrange("p (f c) -> p f c", f=FT),
                             w2_v[bass.ds(e, 1)].rearrange("a p f c -> (a p) f c")).then_inc(w2_in, 16)

            def load_row(dst, rows_d, e, b, came):
                src = rows_d.rearrange("(b e) n -> b e n", b=B)[b][bass.ds(e, 1), :]
                sp.dma_start(dst[:, b * N:(b + 1) * N],
                             src.rearrange("a n -> (a n)").partition_broadcast(P)).then_inc(came[b], 16)

            sp.wait_ge(at_split, H * TPH)
            load_w1(0)
            load_w2(0)
            sp.wait_ge(rows_copied, 2)
            sp.dma_start(w_dram, rows[0:P:REP, :]).then_inc(w_stored, 16)
            sp.wait_ge(tie_step, 8)
            sp.dma_start(slot_dram, cum[0:P:REP, :]).then_inc(slots_stored, 16)
            sp.wait_ge(slots_stored, 16)
            sp.wait_ge(slot_tok_ready, 1)
            for b in range(B):
                load_row(slot_of, slot_dram, 0, b, slots_in)
            sp.wait_ge(w_stored, 16)
            for b in range(B):
                load_row(weights, w_dram, 0, b, w_in)

            def next_w1(e):
                sp.wait_ge(w1_split, e)
                load_w1(e)

            def next_w2(e):
                sp.wait_ge(w2_split, e)
                load_w2(e)

            def next_slots(e):
                for b in range(B):
                    sp.wait_ge(sca_ready, 2 * (e - 1) + b + 1)
                    load_row(slot_of, slot_dram, e, b, slots_in)

            def next_weights(e):
                for b in range(B):
                    sp.wait_ge(prod_ready, NCH * (B * (e - 1) + b + 1))
                    load_row(weights, w_dram, e, b, w_in)

            for e in (1, 2):
                next_w1(e)
                next_w2(e)
            next_slots(1)
            with sp.Fori(1, E - 2) as e:
                next_w1(e + 2)
                next_weights(e)
                next_w2(e + 2)
                next_slots(e + 1)
            next_weights(E - 2)
            next_slots(E - 1)
            next_weights(E - 1)
            for b in range(B):
                sp.wait_ge(ln_done, B + b + 1)
                sp.dma_start(out[b].rearrange("(t p) d -> p t d", p=P),
                             x1[:, b * QT:(b + 1) * QT, :]).then_inc(out_done, 16)
            sp.wait_ge(out_done, 16 * B)

        @block.gpsimd
        def _(pool):
            pool.memset(ident[:, :], 0.0).then_inc(const_ready, 1)
            pool.memset(ones[:, :], 1.0).then_inc(const_ready, 1)
            pool.memset(neg_half[:, :], -0.5).then_inc(const_ready, 1)
            pool.memset(eps_c[:, :], EPS * DV).then_inc(const_ready, 1)
            pool.wait_ge(const_ready, 4)
            pool.affine_select(out=ident[:, :], in_=ident[:, :], compare_op=ALU.not_equal, fill=1.0, base=0,
                               pattern=[[-1, P]], channel_multiplier=1).then_inc(const_ready, 1)
            pool.memset(ln_eps[:, :], EPS * D).then_inc(eps_ready, 1)
            pool.wait_ge(eps_ready, 1)

            def ln_factors(n):
                c = slice((n % B) * QT, (n % B + 1) * QT)
                pool.wait_ge(ln_ssq, n + 1)
                pool.tensor_tensor(stat[:, 1, c], stat[:, 1, c], ln_eps[:, c], ALU.add).then_inc(ln_var, 1)
                pool.wait_ge(ln_var, n + 1)
                pool.tensor_tensor(stat[:, 2, c], stat[:, 1, c], neg_half[:, c], ALU.pow).then_inc(ln_fac, 1)

            for b in range(B):
                pool.wait_ge(xk_hi_done, b + 1)
                s = slice(b * QT, (b + 1) * QT)
                pool.tensor_tensor(xk_lo[:, s, :], xres[:, s, :], xk_hi[:, s, :].bitcast(F32),
                                   ALU.subtract).then_inc(xk_split, 1)

            def slot(h, i, first, last, tail):
                t = TPH * h + i
                r = i - LAG_T
                if exists(h, r, first) and r < (TPH - 1 if last else TPH):
                    tt, par, g = t - LAG_T, r % 2, (r // GT) % 2
                    need(pool, t_copied, tt + 1)
                    gabs = GPH * h + r // GT
                    if not (first and r // GT < 2):
                        pool.wait_ge(u_ready, gabs - 1)
                    s1 = psum1[:, r % TPH:r % TPH + 1]
                    pool.tensor_tensor(s1sq[:, r % TPH:r % TPH + 1], s1, s1, ALU.mult).then_inc(s1sq_ready, 1)
                    c = slice((r % GT) * P, (r % GT + 1) * P)
                    src = at32[:, par, :].rearrange("p (k q) -> p k q", q=P)
                    pool.tensor_scalar(at_hi[:, g, :, c], src, 1.0, 0.0, ALU.mult, ALU.add).then_inc(at_hi_done, 1)
                r = i - LAG_O
                if exists(h, r, first) and r < TPH:
                    tt, par = t - LAG_O, r % 2
                    if last and r == TPH - 1:
                        pool.wait_ge(s1sq_last, 1)
                    else:
                        pool.wait_ge(s1sq_ready, tt + 1)
                    need(pool, var_ready, tt - 1)
                    pool.tensor_tensor(es1[:, par:par + 1], s1sq[:, r % TPH:r % TPH + 1], eps_c[:, 0:1],
                                       ALU.mult).then_inc(es1_ready, 1)
                    pool.wait_ge(es1_ready, tt + 1)
                    pool.wait_ge(ssq_ready, tt + 1)
                    pool.tensor_tensor(var_o[:, par:par + 1], ssq[:, par:par + 1], es1[:, par:par + 1],
                                       ALU.add).then_inc(var_ready, 1)
                    need(pool, y_added, tt - 1)
                    pool.wait_ge(var_ready, tt + 1)
                    pool.tensor_tensor(fac[:, par:par + 1], var_o[:, par:par + 1], neg_half[:, 0:1],
                                       ALU.pow).then_inc(fac_ready, 1)
                r = i - LAG_T
                if exists(h, r, first) and r < (TPH - 1 if last else TPH):
                    tt = t - LAG_T
                    pool.wait_ge(at_hi_done, tt + 1)
                    pool.tensor_tensor(at_lo[:, g, :, c], src, at_hi[:, g, :, c].bitcast(F32),
                                       ALU.subtract).then_inc(at_split, 1)
                if tail and i == AT_LN[3]:
                    ln_factors(0)

            heads(pool, slot)

            pool.memset(grp[:, :], 1.0).then_inc(topk_const, 1)
            pool.memset(base[:, :], 0).then_inc(topk_const, 1)
            pool.memset(pw[:, :], float(2 ** (LB * (LEVELS - 1)))).then_inc(topk_const, 1)
            pool.iota(jcur[:, :], pattern=[[0, 1]], base=0, channel_multiplier=1).then_inc(topk_const, 1)
            by_group = grp[:, :].rearrange("p (g j) -> p g j", j=REP)
            pool.wait_ge(topk_const, 4)
            pool.affine_select(out=by_group, in_=by_group, compare_op=ALU.is_ge, fill=0.0, base=0,
                               pattern=[[-REP, R], [0, REP]], channel_multiplier=1).then_inc(topk_const, 1)
            pool.wait_ge(topk_const, 5)
            pool.affine_select(out=by_group, in_=by_group, compare_op=ALU.is_ge, fill=0.0, base=REP - 1,
                               pattern=[[REP, R], [0, REP]], channel_multiplier=-1).then_inc(topk_const, 1)
            pool.iota(slot_row_i[:, :], pattern=[[1, CAP]], base=1, channel_multiplier=0).then_inc(topk_const, 1)
            pool.iota(slot_col_i[:, :], pattern=[[P, CT]], base=1, channel_multiplier=1).then_inc(topk_const, 1)
            for n in range(1, B):
                ln_factors(n)
            for b in range(B):
                s = slice(b * QT, (b + 1) * QT)
                pool.wait_ge(x1_hi_done, b + 1)
                pool.tensor_tensor(x1_lo[:, s, :], x1[:, s, :], x1_hi[:, s, :].bitcast(F32),
                                   ALU.subtract).then_inc(x1_split, 1)

            def w_lower(raw, hi, lo, hi_done, split, e):
                pool.wait_ge(hi_done, e + 1)
                pool.tensor_tensor(lo, raw.rearrange("p (f c) -> p f c", c=P), hi.bitcast(F32),
                                  ALU.subtract).then_inc(split, 1)

            w_lower(w1_raw, w1_hi, w1_lo, w1_hi_done, w1_split, 0)
            w_lower(w2_raw, w2_hi, w2_lo, w2_hi_done, w2_split, 0)

            def add_out(e, ks):
                for k in ks:
                    n = B * NCH * e + k
                    if is_at(e, E - 1) and k % 2:
                        continue
                    pool.wait_ge(prod_ready, n + 1)
                    c = slice(k * NC, (k + 1) * NC)
                    pool.tensor_tensor(acc_t[:, c], acc_t[:, c], prod[:, k % 2, :], ALU.add).then_inc(acc_added, 1)

            def ffn(e, first, tail):
                if not tail:
                    for f in range(FD, FT):
                        pool.wait_ge(g_hi_done, FT * e + f + 1)
                        pool.tensor_tensor(g_lo[:, f, :], gelu[:, f, :], g_hi[:, f, :].bitcast(F32),
                                           ALU.subtract).then_inc(g_split_p, 1)
                    if not is_at(e, E - 1):
                        w_lower(w1_raw, w1_hi, w1_lo, w1_hi_done, w1_split, e + 1)
                if not first:
                    add_out(e - 1, range(NCH))
                if not tail and not is_at(e, E - 1):
                    w_lower(w2_raw, w2_hi, w2_lo, w2_hi_done, w2_split, e + 1)
                if not first:
                    add_out(e - 1, range(NCH, B * NCH))

            experts(pool, ffn)
            for n in range(B, 2 * B):
                ln_factors(n)

        @block.scalar
        def _(act):
            for b in range(B):
                act.wait_ge(xt_ready, b + 1)
                act.activation(xt_hi[:, b * N:(b + 1) * N], ring[b][:, :], ACT.Copy).then_inc(xt_hi_done, 1)
            def q_round(h, which, maps=(0, 1)):
                for m in maps:
                    b = 1 if which == "b" else 0
                    for c in range(NCH):
                        cols = slice(c * NC, (c + 1) * NC)
                        act.wait_ge(q_ready, NCH * q_index(h, which, m) + c + 1)
                        act.activation(q_hi[:, b, m, cols], ring[m][:, cols], ACT.Copy).then_inc(q_hi_done, 1)

            def ln_squares(n):
                b = n % B
                act.wait_ge(ln_cent, n + 1)
                act.activation(sq[:, b * QT:(b + 1) * QT, :], x1[:, b * QT:(b + 1) * QT, :],
                               ACT.Square).then_inc(ln_sq, 1)

            q_round(0, "a")
            act.wait_ge(lam_sum, 2)
            act.activation(lam_s[:, 2:4], lam_s[:, 0:2], ACT.Exp).then_inc(lam_exp, 1)

            def slot(h, i, first, last, tail):
                t = TPH * h + i

                def q_rounds(m):
                    if not tail and i == AT_QB[m]:
                        q_round(h, "b", (m,))
                    if not last and i == AT_QA[m]:
                        q_round(h + 1, "a", (m,))

                r = i - LAG_O
                if r % GT == 0 and exists(h, r, first) and r < TPH:
                    g = GPH * h + r // GT
                    need(act, u_ready, g + 1)
                    need(act, o_ready, GT * g)
                    act.activation(u_hi[:, :], u_ps[:, :], ACT.Copy).then_inc(u_hi_done, 1)
                if not tail and i == AT_WW:
                    act.wait_ge(wp_split, h + 1)
                    act.wait_ge(wt_split, 3 * (h + 1))
                    need(act, o_ready, t - AT_WW)
                    act.activation(ww_hi[:, :], wwn_hi[:, :].bitcast(F32), ACT.Copy).then_inc(ww_installed, 1)
                    act.activation(ww_lo[:, :], wwn_lo[:, :].bitcast(F32), ACT.Copy).then_inc(ww_installed, 1)
                if not tail:
                    par = i % 2
                    for m in range(2):
                        need(act, negmax_ready, 2 * t + m + 1)
                        need(act, attn_ready, t - 1)
                        if m == 0:
                            need(act, s1sq_ready, t - TPH + 1)
                        sums = psum1[:, i:i + 1] if m == 0 else psum2[:, par:par + 1]
                        act.activation(prob[:, par, m, :], ring[m][:, :], ACT.Exp, bias=negmax[:, par, m:m + 1],
                                       accum_out=sums).then_inc(prob_ready, 1)
                q_rounds(0)
                r = i - LAG_T
                if exists(h, r, first) and r < TPH:
                    tt = t - LAG_T
                    act.wait_ge(t_ready, tt + 1)
                    need(act, at_split, tt - 1)
                    act.activation(at32[:, r % 2, :], t_ps[:, :], ACT.Copy).then_inc(t_copied, 1)
                q_rounds(1)
                r = i - LAG_O
                if exists(h, r, first) and r < TPH:
                    tt, par = t - LAG_O, r % 2
                    act.wait_ge(o_ready, tt + 1)
                    need(act, var_ready, tt - 1)
                    need(act, ssq_ready, tt - 1)
                    act.activation(osq[:, par, :], o_bank(r, last)[:, 0:DV], ACT.Square,
                                   accum_out=ssq[:, par:par + 1]).then_inc(ssq_ready, 1)
                if tail and i == AT_LN[1]:
                    ln_squares(0)

            heads(act, slot)

            for b in range(B):
                if b > 0:
                    ln_squares(b)
                act.wait_ge(x1t_ready, b + 1)
                act.activation(acc_t[:, b * N:(b + 1) * N], x1t_ps[b][:, :], ACT.Copy).then_inc(x1t_copied, 1)
            for b in range(B):
                s = slice(b * QT, (b + 1) * QT)
                act.activation(x1_hi[:, s, :], x1[:, s, :], ACT.Copy).then_inc(x1_hi_done, 1)
            act.wait_ge(gate_step, 2)
            act.activation(pr[:, :, :], pr[:, :, :], ACT.Exp).then_inc(gate_exp, 1)
            act.activation(gelu_first[:, :], eps_c[:, :], ACT.Gelu).then_inc(ticked, 1)

            def w_round(raw, hi, came, used, hi_done, e):
                act.wait_ge(came, 16 * (e + 1))
                if not is_at(e, 0):
                    act.wait_ge(*used)
                act.activation(hi, raw.rearrange("p (f c) -> p f c", c=P), ACT.Copy).then_inc(hi_done, 1)

            def xs_copy(e):
                for part, (dst, src) in enumerate(((xs_hi, u_ps), (xs_lo, o_ps))):
                    act.wait_ge(xs_ready, 2 * (e + 1))
                    if part == 0 and not is_at(e, 0):
                        act.wait_ge(up_ready, FT * e)
                    act.activation(dst[:, :], src[:, :], ACT.Copy).then_inc(xs_copied, 1)

            w_round(w1_raw, w1_hi, w1_in, None, w1_hi_done, 0)
            w_round(w2_raw, w2_hi, w2_in, None, w2_hi_done, 0)
            act.wait_ge(rows_ready, 1)
            act.activation(rows[:, NC:N], t_ps[:, NC:N], ACT.Copy).then_inc(rows_copied, 1)
            xs_copy(0)

            def ffn(e, first, tail):
                if tail:
                    return
                for f in range(FT + 1):
                    if f < FT:
                        act.wait_ge(up_ready, FT * e + f + 1)
                        if f < FD:
                            need(act, g_split, FD * (e - 1) + f + 1)
                        else:
                            need(act, g_split_p, (FT - FD) * (e - 1) + f - FD + 1)
                        act.activation(gelu[:, f, :], up_bank(f), ACT.Gelu).then_inc(gelu_ready, 1)
                    if f > 0:
                        act.wait_ge(gelu_ready, FT * e + f)
                        need(act, down_ready, e)
                        act.activation(g_hi[:, f - 1, :], gelu[:, f - 1, :], ACT.Copy).then_inc(g_hi_done, 1)
                if not is_at(e, E - 1):
                    w_round(w1_raw, w1_hi, w1_in, (up_ready, FT * (e + 1)), w1_hi_done, e + 1)
                    xs_copy(e + 1)
                act.wait_ge(down_ready, e + 1)
                need(act, y_ready, e)
                act.activation(yt, t_ps[:, 0:SL], ACT.Copy).then_inc(yt_copied, 1)
                if not is_at(e, E - 1):
                    w_round(w2_raw, w2_hi, w2_in, (down_ready, e + 1), w2_hi_done, e + 1)
                act.wait_ge(y_ready, e + 1)
                if not is_at(e, E - 1):
                    need(act, out_ready, B * NCH * e)
                act.activation(y_parts(e)[0], t_ps[:, NC:NC + SL].rearrange("p (s d) -> p s d", d=D),
                               ACT.Copy).then_inc(y_hi_done, 1)

            experts(act, ffn)
            for n in range(B, 2 * B):
                ln_squares(n)

        @block.vector
        def _(dve):
            for b in range(B):
                dve.wait_ge(x_in[b], 16)
                s = slice(b * QT, (b + 1) * QT)
                dve.tensor_copy(xk_hi[:, s, :], xres[:, s, :]).then_inc(xk_hi_done, 1)
            for b in range(B):
                c = slice(b * N, (b + 1) * N)
                dve.wait_ge(xt_hi_done, b + 1)
                dve.tensor_tensor(xt_lo[:, c], ring[b][:, :], xt_hi[:, c].bitcast(F32),
                                  ALU.subtract).then_inc(xt_split, 1)

            def m_parts(h):
                dve.wait_ge(m_ready, h + 1)
                src = ring[0][:, 0:2 * D].rearrange("p (m d) -> p m d", m=2)
                dve.tensor_scalar(m_hi[:, :, :], src, SCALE, None, ALU.mult).then_inc(m_hi_done, 1)
                dve.wait_ge(m_hi_done, h + 1)
                dve.scalar_tensor_tensor(out=m_lo[:, :, :], in0=src, scalar=SCALE, in1=m_hi[:, :, :].bitcast(F32),
                                         op0=ALU.mult, op1=ALU.subtract).then_inc(m_split, 1)

            def q_parts(h, which, maps=(0, 1)):
                for m in maps:
                    b = 1 if which == "b" else 0
                    for c in range(NCH):
                        cols = slice(c * NC, (c + 1) * NC)
                        dve.wait_ge(q_hi_done, NCH * q_index(h, which, m) + c + 1)
                        dve.tensor_tensor(q_lo[:, b, m, cols], ring[m][:, cols], q_hi[:, b, m, cols].bitcast(F32),
                                          ALU.subtract).then_inc(q_split, 1)

            def layer_norm(n):
                b = n % B
                s = slice(b * QT, (b + 1) * QT)
                rows_n = x1[:, s, :]
                src = rows_n if n < B else ring[b][:, :].rearrange("p (t d) -> p t d", d=D)

                def wide(a):
                    return a.unsqueeze(2).broadcast_to([P, QT, D])

                dve.reduce_sum(stat[:, 0, s], src, AX.X).then_inc(ln_sum, 1)
                dve.wait_ge(ln_sum, n + 1)
                dve.tensor_scalar(stat[:, 3, s], stat[:, 0, s], 1.0 / D, None, ALU.mult).then_inc(ln_mean, 1)
                dve.wait_ge(ln_mean, n + 1)
                dve.tensor_tensor(rows_n, src, wide(stat[:, 3, s]), ALU.subtract).then_inc(ln_cent, 1)

            def layer_norm_sums(n):
                s = slice((n % B) * QT, (n % B + 1) * QT)
                dve.wait_ge(ln_sq, n + 1)
                dve.reduce_sum(stat[:, 1, s], sq[:, s, :], AX.X).then_inc(ln_ssq, 1)

            def layer_norm_end(n):
                s = slice((n % B) * QT, (n % B + 1) * QT)
                dve.wait_ge(ln_fac, n + 1)
                dve.scalar_tensor_tensor(out=x1[:, s, :], in0=x1[:, s, :], scalar=math.sqrt(D),
                                         in1=stat[:, 2, s].unsqueeze(2).broadcast_to([P, QT, D]),
                                         op0=ALU.mult, op1=ALU.mult).then_inc(ln_done, 1)

            m_parts(0)
            q_parts(0, "a")

            dve.wait_ge(lam_in_s, 64)
            for n in range(2):
                dve.tensor_tensor(lam_pr[:, n, :], lam_in[:, 2 * n, :], lam_in[:, 2 * n + 1, :],
                                  ALU.mult).then_inc(lam_prod, 1)
            for n in range(2):
                dve.wait_ge(lam_prod, n + 1)
                dve.reduce_sum(lam_s[:, n:n + 1], lam_pr[:, n, :], AX.X).then_inc(lam_sum, 1)
            dve.wait_ge(lam_exp, 1)
            dve.tensor_tensor(lam_s[:, 0:1], lam_s[:, 3:4], lam_s[:, 2:3], ALU.subtract).then_inc(lam_sum, 1)
            dve.wait_ge(lam_sum, 3)
            dve.tensor_scalar(lam_s[:, 1:2], lam_s[:, 0:1], -LAMBDA_INIT, None, ALU.add).then_inc(lam_sum, 1)
            dve.wait_ge(lam_sum, 4)
            dve.wait_ge(const_ready, 5)
            dve.tensor_scalar(lam_d[:, :], ident[0:H, 0:H], lam_s[:, 1:2], None, ALU.mult).then_inc(lam_diag, 1)

            def slot(h, i, first, last, tail):
                t = TPH * h + i
                par = i % 2

                def head_lambda():
                    need(dve, coef_ready, t)
                    dve.tensor_copy(neglam_h[:, :], neglam[:, bass.ds(h, 1)]).then_inc(lam_head, 1)

                if i == 0 and not first:
                    head_lambda()

                def row_max(m):
                    dve.wait_ge(scores_ready, 2 * t + m + 1)
                    need(dve, prob_ready, 2 * (t - 2) + m + 1)
                    dve.tensor_reduce(negmax[:, par, m:m + 1], ring[m][:, :], axis=AX.X, op=ALU.max,
                                      negate=True).then_inc(negmax_ready, 1)

                if not tail:
                    row_max(0)
                r = i - LAG_O
                if r % GT == 0 and exists(h, r, first) and r < TPH:
                    g = GPH * h + r // GT
                    dve.wait_ge(u_hi_done, g + 1)
                    dve.tensor_tensor(u_lo[:, :], u_ps[:, :], u_hi[:, :].bitcast(F32),
                                      ALU.subtract).then_inc(u_split, 1)
                if not tail:
                    row_max(1)
                if first and i == 0:
                    dve.wait_ge(lam_ps, 1)
                    dve.tensor_copy(neglam[:, :], o_ps[:, 0:H]).then_inc(lam_ready, 1)
                    dve.wait_ge(rms_in, 16)
                    dve.tensor_scalar(rms_c[:, :], rms_raw[:, :], (1.0 - LAMBDA_INIT) * math.sqrt(DV), None,
                                      ALU.mult).then_inc(rms_ready, 1)
                    dve.wait_ge(rms_ready, 1)
                    dve.wait_ge(lam_ready, 1)
                    head_lambda()
                r = i - LAG_Y
                if exists(h, r, first) and r < TPH:
                    tt = t - LAG_Y
                    dve.wait_ge(fac_ready, tt + 1)
                    dst = xres[:, r % TPH, :]
                    dve.scalar_tensor_tensor(out=dst, in0=o_bank(r, last)[:, DV:WWN], scalar=fac[:, r % 2:r % 2 + 1],
                                             in1=dst, op0=ALU.mult, op1=ALU.add).then_inc(y_added, 1)

                def q_lower(m):
                    if not tail and i == AT_QB[m]:
                        q_parts(h, "b", (m,))
                    if not last and i == AT_QA[m]:
                        q_parts(h + 1, "a", (m,))

                q_lower(0)
                if not last and i == AT_M:
                    m_parts(h + 1)
                if not tail and i == AT_WP:
                    dve.wait_ge(wp_ready, h + 1)
                    dve.tensor_copy(wwn_hi[:, DV:WWN], ring[0][:, 0:D]).then_inc(wp_hi_done, 1)
                    dve.wait_ge(wp_hi_done, h + 1)
                    dve.tensor_tensor(wwn_lo[:, DV:WWN], ring[0][:, 0:D], wwn_hi[:, DV:WWN].bitcast(F32),
                                      ALU.subtract).then_inc(wp_split, 1)
                if not tail and i == AT_WT:
                    dve.wait_ge(wt_ready, h + 1)
                    need(dve, ww_installed, 2 * h)
                    dve.tensor_copy(wwn_hi[:, 0:DV], ring[1][:, 0:DV]).then_inc(wt_hi_done, 1)
                    dve.wait_ge(wt_hi_done, h + 1)
                    dve.tensor_tensor(wwn_lo[:, 0:DV], ring[1][:, 0:DV], wwn_hi[:, 0:DV].bitcast(F32),
                                      ALU.subtract).then_inc(wt_split, 1)
                    for m in range(2):
                        dve.tensor_scalar(wot_s[:, m, :], ring[1][:, NC + m * D:NC + (m + 1) * D],
                                          rms_c[:, m:m + 1], None, ALU.mult).then_inc(wt_split, 1)
                if not tail:
                    dve.wait_ge(prob_ready, 2 * t + 2)
                    if i == 0:
                        dve.wait_ge(lam_head, h + 1)
                    dve.reciprocal(rs2[:, par:par + 1], psum2[:, par:par + 1]).then_inc(rs2_ready, 1)
                    dve.wait_ge(rs2_ready, t + 1)
                    dve.tensor_scalar(coef[:, par:par + 1], rs2[:, par:par + 1], psum1[:, i:i + 1],
                                      neglam_h[:, :], ALU.mult, ALU.mult).then_inc(coef_ready, 1)
                    dve.wait_ge(coef_ready, t + 1)
                    need(dve, t_ready, t - 1)
                    dve.scalar_tensor_tensor(out=attn[:, par, :], in0=prob[:, par, 1, :],
                                             scalar=coef[:, par:par + 1], in1=prob[:, par, 0, :],
                                             op0=ALU.mult, op1=ALU.add).then_inc(attn_ready, 1)
                q_lower(1)
                if tail and i == TPH - 1 + LAG_T:
                    g, c = (TPH // GT - 1) % 2, slice((GT - 1) * P, GT * P)
                    src = at32[:, (TPH - 1) % 2, :].rearrange("p (k q) -> p k q", q=P)
                    s1 = psum1[:, TPH - 1:TPH]
                    dve.wait_ge(u_ready, GPH * (H - 1) + TPH // GT - 2)
                    dve.wait_ge(t_copied, H * TPH)
                    dve.tensor_copy(at_hi[:, g, :, c], src).then_inc(last_hi_done, 1)
                    dve.tensor_tensor(s1sq[:, TPH - 1:TPH], s1, s1, ALU.mult).then_inc(s1sq_last, 1)
                    dve.wait_ge(last_hi_done, 1)
                    dve.tensor_tensor(at_lo[:, g, :, c], src, at_hi[:, g, :, c].bitcast(F32),
                                      ALU.subtract).then_inc(at_split, 1)
                if tail and i == AT_LN[0]:
                    dve.wait_ge(y_added, TPH * (H - 1) + QT)
                    layer_norm(0)
                if tail and i == AT_LN[2]:
                    layer_norm_sums(0)
                if tail and i == AT_LN[4]:
                    layer_norm_end(0)

            heads(dve, slot)

            dve.wait_ge(y_added, H * TPH)
            layer_norm(1)
            layer_norm_sums(1)
            layer_norm_end(1)

            dve.wait_ge(topk_const, 8)
            dve.tensor_copy(slot_row[:, :], slot_row_i[:, :]).then_inc(slot_tok_copied, 1)
            dve.tensor_copy(slot_col[:, :], slot_col_i[:, :]).then_inc(slot_tok_copied, 1)
            dve.tensor_scalar(jcur[:, :], jcur[:, :], REP - 1, LB * (LEVELS - 1), ALU.bitwise_and,
                              ALU.logical_shift_left).then_inc(next_ready, 1)

            lg = o_ps[:, 0:QT * R].rearrange("p (t b e) -> p (t b) e", b=B, e=E)
            pv = pr[:, :, :].rearrange("p t (b e) -> p (t b) e", e=E)

            def over_e(a):
                return a.unsqueeze(2).broadcast_to([P, TPH, E])

            dve.wait_ge(gate_ready, 1)
            dve.tensor_reduce(pst[:, 0, :], lg, axis=AX.X, op=ALU.max).then_inc(gate_step, 1)
            dve.wait_ge(gate_step, 1)
            dve.tensor_tensor(pv, lg, over_e(pst[:, 0, :]), ALU.subtract).then_inc(gate_step, 1)
            dve.wait_ge(gate_exp, 1)
            dve.reduce_sum(pst[:, 1, :], pv, AX.X).then_inc(gate_step, 1)
            dve.wait_ge(gate_step, 3)
            dve.reciprocal(pst[:, 2, :], pst[:, 1, :]).then_inc(gate_step, 1)
            dve.wait_ge(gate_step, 4)
            dve.tensor_tensor(pr_rep.rearrange("p (t e j) -> p t e j", e=E, j=REP),
                              pv.unsqueeze(3).broadcast_to([P, TPH, E, REP]),
                              pst[:, 2, :].unsqueeze(2).unsqueeze(3).broadcast_to([P, TPH, E, REP]),
                              ALU.mult).then_inc(gate_step, 1)
            dve.wait_ge(rows_ready, 1)
            dve.tensor_copy(rows[:, 0:NC], t_ps[:, 0:NC]).then_inc(rows_copied, 1)

            dve.wait_ge(rows_copied, 2)
            dve.wait_ge(next_ready, 1)
            dve.tensor_tensor(cand[:, :], base[:, :], jcur[:, :], ALU.bitwise_or).then_inc(cand_ready, 1)

            def level(lv):
                dve.wait_ge(cand_ready, lv + 1)
                dve.tensor_scalar(tie, rows, cand[:, :].bitcast(F32), None, ALU.is_ge, ALU.add,
                                  accum_out=cnt[:, :]).then_inc(cnt_ready, 1)
                dve.tensor_scalar(jcur[:, :], jcur[:, :], LB, None,
                                  ALU.logical_shift_right).then_inc(next_ready, 1)
                dve.wait_ge(cnt_ready, lv + 1)
                dve.tensor_scalar(hit[:, :], cnt[:, :], CAP - 0.5, None, ALU.is_ge).then_inc(hit_ready, 1)
                dve.wait_ge(next_ready, 4 * lv + 2)
                dve.tensor_tensor(base_j[:, :], base[:, :], jcur[:, :], ALU.bitwise_or).then_inc(next_ready, 1)
                dve.wait_ge(votes_ready, lv + 1)
                dve.tensor_scalar(step[:, :], u_ps[:, 0:1], -1.0, pw[:, :], ALU.add,
                                  ALU.mult).then_inc(step_ready, 1)
                dve.wait_ge(next_ready, 4 * lv + 3)
                dve.wait_ge(step_ready, lv + 1)
                dve.tensor_tensor(cand[:, :], base_j[:, :], step[:, :], ALU.bitwise_or).then_inc(cand_ready, 1)
                dve.tensor_tensor(base[:, :], base[:, :], step[:, :], ALU.bitwise_or).then_inc(next_ready, 1)
                dve.tensor_scalar(pw[:, :], pw[:, :], 1.0 / REP, None, ALU.mult).then_inc(next_ready, 1)

            with dve.Fori(0, LEVELS // LEVELS_PT) as turn:
                for k in range(LEVELS_PT):
                    level(LEVELS_PT * turn + k)
            dve.wait_ge(next_ready, 1 + 4 * LEVELS)
            thr = base[:, :].bitcast(F32)
            dve.tensor_scalar(tie, rows, thr, None, ALU.is_gt, ALU.add, accum_out=cnt_gt[:, :]).then_inc(tie_step, 1)
            dve.wait_ge(tie_step, 1)
            dve.tensor_scalar(free_n[:, :], cnt_gt[:, :], -1.0, float(CAP), ALU.mult, ALU.add).then_inc(tie_step, 1)
            dve.tensor_scalar(tie, rows, thr, None, ALU.is_equal).then_inc(tie_step, 1)
            dve.wait_ge(tie_step, 3)
            dve.tensor_tensor_scan(cum, tie, tie, 0.0, ALU.add, ALU.max).then_inc(tie_step, 1)
            dve.wait_ge(tie_step, 4)
            dve.scalar_tensor_tensor(out=tie, in0=cum, scalar=free_n[:, :], in1=tie, op0=ALU.is_gt,
                                     op1=ALU.mult).then_inc(tie_step, 1)
            dve.wait_ge(tie_step, 5)
            dve.scalar_tensor_tensor(out=tie, in0=rows, scalar=thr, in1=tie, op0=ALU.is_ge,
                                     op1=ALU.subtract).then_inc(tie_step, 1)
            dve.wait_ge(tie_step, 6)
            dve.tensor_tensor_scan(cum, tie, tie, 0.0, ALU.add, ALU.max).then_inc(tie_step, 1)
            dve.wait_ge(tie_step, 7)
            dve.tensor_tensor(cum, cum, tie, ALU.mult).then_inc(tie_step, 1)

            def gather_ones(e, tiles=range(B * QT)):
                for b, j in (divmod(k, QT) for k in tiles):
                    if j == 0:
                        if not is_at(e, 0):
                            dve.wait_ge(gat_ready, 2 * (e - 1) + b + 1)
                            dve.wait_ge(xs_ready, 2 * (e - 1) + b + 1)
                        dve.tensor_copy(slot_e[:, :, b:b + 1], slot_tok[:, :, bass.ds(b * E + e, 1)]
                                        ).then_inc(slot_e_ready, 1)
                        dve.wait_ge(slot_e_ready, 2 * e + b + 1)
                    last_c = dve.tensor_scalar(gat[:, b, j, :], slot_row[:, :], slot_e[:, j, b:b + 1], None,
                                               ALU.is_equal)
                    if j == QT - 1:
                        last_c.then_inc(gat_ready, 1)

            def scatter_ones(e, bs=range(B)):
                for b in bs:
                    dve.wait_ge(slots_in[b], 16 * (e + 1))
                    if not is_at(e, E - 1):
                        need(dve, out_ready, B * NCH * (e - 1) + NCH * (b + 1))
                    dve.tensor_copy(tick[:, b:b + 1], slot_col[:, 0:1]).then_inc(ticked, 1)
                    for j in range(CT):
                        last_c = dve.tensor_scalar(sca_of(e)[:, b, j, :], slot_of[:, b * N:(b + 1) * N],
                                                   slot_col[:, j:j + 1], None, ALU.is_equal)
                    last_c.then_inc(sca_ready, 1)

            def y_lower(e):
                dve.wait_ge(y_hi_done, e + 1)
                dve.tensor_tensor(y_parts(e)[1], t_ps[:, NC:NC + SL].rearrange("p (s d) -> p s d", d=D),
                                  y_parts(e)[0].bitcast(F32), ALU.subtract).then_inc(y_split, 1)

            def weighted(e, ks=range(B * NCH)):
                for k in ks:
                    n, b = B * NCH * e + k, k // NCH
                    if k % NCH == 0:
                        dve.wait_ge(w_in[b], 16 * (e + 1))
                    dve.wait_ge(out_ready, n + 1)
                    if is_at(e, E - 1) and k > 1:
                        if k % 2:
                            dve.wait_ge(acc_added_dve, k // 2)
                        else:
                            dve.wait_ge(acc_added, B * NCH * e + k // 2)
                    else:
                        need(dve, acc_added, n - 1)
                    dve.tensor_tensor(prod[:, k % 2, :], ring[1][:, (k % 2) * NC:(k % 2 + 1) * NC],
                                      weights[:, k * NC:(k + 1) * NC], ALU.mult).then_inc(prod_ready, 1)
                    if is_at(e, E - 1) and k % 2:
                        c = slice(k * NC, (k + 1) * NC)
                        dve.wait_ge(prod_ready, n + 1)
                        dve.wait_ge(acc_added, B * NCH * e)
                        dve.tensor_tensor(acc_t[:, c], acc_t[:, c], prod[:, 1, :],
                                          ALU.add).then_inc(acc_added_dve, 1)

            dve.wait_ge(slot_tok_ready, 1)
            dve.tensor_copy(slot_tok[:, :, :], t_ps[:, :].rearrange("p (t r j) -> p t r j", r=R, j=REP)[:, :, :, 0]
                            ).then_inc(slot_tok_copied, 1)
            dve.wait_ge(slot_tok_copied, 3)
            gather_ones(0)
            gather_ones(1)

            def ffn(e, first, tail):
                if not tail:
                    for f in range(FD):
                        dve.wait_ge(g_hi_done, FT * e + f + 1)
                        dve.tensor_tensor(g_lo[:, f, :], gelu[:, f, :], g_hi[:, f, :].bitcast(F32),
                                          ALU.subtract).then_inc(g_split, 1)
                    if not is_at(e, E - 2) and not is_at(e, E - 1):
                        if first:
                            gather_ones(e + 2)
                        else:
                            gather_ones(e + 2, range(GAT_SPLIT))
                            weighted(e - 1, range(NCH))
                            gather_ones(e + 2, range(GAT_SPLIT, B * QT))
                            weighted(e - 1, range(NCH, B * NCH))
                if is_at(e, E - 1):
                    scatter_ones(e - 1)
                    weighted(e - 1, range(NCH))
                    y_lower(e)
                    scatter_ones(e, (0,))
                    weighted(e - 1, range(NCH, B * NCH))
                    scatter_ones(e, range(1, B))
                    return
                if is_at(e, E - 2) or tail:
                    weighted(e - 1)
                if not tail:
                    y_lower(e)
                    if not is_at(e, E - 2):
                        scatter_ones(e)

            experts(dve, ffn)
            for n in range(B, 2 * B):
                dve.wait_ge(back_ready, n - B + 1)
                layer_norm(n)
            for n in range(B, 2 * B):
                layer_norm_sums(n)
            for n in range(B, 2 * B):
                layer_norm_end(n)

        @block.tensor
        def _(pe):
            pe.wait_ge(const_ready, 5)
            for b in range(B):
                pe.wait_ge(x_in[b], 16)
                for j in range(QT):
                    last_t = pe.transpose(ring[b][:, j * P:(j + 1) * P], xres[:, b * QT + j, :], ident[:, :])
                last_t.then_inc(xt_ready, 1)

            def three(dst, a_hi, a_lo, b_hi, b_lo, start=True, stop=True):
                pe.matmul(dst, a_hi, b_hi, start=start, stop=False)
                pe.matmul(dst, a_hi, b_lo, start=False, stop=False)
                return pe.matmul(dst, a_lo, b_hi, start=False, stop=stop)

            def m_product(h):
                pe.wait_ge(qk_in, 32 * (h + 1))
                for m in range(2):
                    last_m = pe.matmul(ring[0][:, m * D:(m + 1) * D], wq_s[:, m, :], wk_s[:, m, :],
                                       start=True, stop=True)
                last_m.then_inc(m_ready, 1)

            def q_product(h, which, maps=(0, 1)):
                b = 1 if which == "b" else 0
                for m in maps:
                    for c in range(NCH):
                        cols = slice(b * N + c * NC, b * N + (c + 1) * NC)
                        three(ring[m][:, c * NC:(c + 1) * NC], m_hi[:, m, :], m_lo[:, m, :],
                              xt_hi[:, cols], xt_lo[:, cols]).then_inc(q_ready, 1)

            pe.wait_ge(xt_split, 1)
            m_product(0)
            pe.wait_ge(xt_split, 2)
            pe.wait_ge(m_split, 1)
            q_product(0, "a")

            def slot(h, i, first, last, tail):
                t = TPH * h + i
                if not tail:
                    b, qt = i // QT, i % QT
                    q = slice(qt * P, (qt + 1) * P)
                    for m in range(2):
                        need(pe, prob_ready, 2 * (t - 1) + m + 1)
                        if i == AT_M + 1 and m == 0 and not last:
                            pe.wait_ge(m_split, h + 2)
                        if i == AT_WT + 1 and m == 1:
                            pe.wait_ge(wt_split, 3 * (h + 1))
                        if i == AT_WP + 1 and m == 0:
                            pe.wait_ge(wp_split, h + 1)
                        if i == 0:
                            pe.wait_ge(q_split, NCH * (q_index(h, "a", m) + 1))
                        if i == QT:
                            pe.wait_ge(q_split, NCH * (q_index(h, "b", m) + 1))
                        for c in range(NCH):
                            if i == AT_QB[m] + 1:
                                pe.wait_ge(q_split, NCH * q_index(h, "b", m) + c + 1)
                            if i == AT_QA[m] + 1 and not last:
                                pe.wait_ge(q_split, NCH * q_index(h + 1, "a", m) + c + 1)
                            cols = slice(b * N + c * NC, b * N + (c + 1) * NC)
                            last_s = three(ring[m][:, c * NC:(c + 1) * NC], q_hi[:, b, m, q], q_lo[:, b, m, q],
                                           xt_hi[:, cols], xt_lo[:, cols])
                        last_s.then_inc(scores_ready, 1)
                if first and i == 0:
                    pe.wait_ge(lam_diag, 1)
                    pe.matmul(o_ps[:, 0:H], ones[0:H, :], lam_d[:, :], start=True, stop=True).then_inc(lam_ps, 1)
                r = i - LAG_T
                if exists(h, r, first) and r < TPH:
                    tt = t - LAG_T
                    pe.wait_ge(attn_ready, tt + 1)
                    need(pe, t_copied, tt)
                    for k in range(KT):
                        last_t = pe.transpose(t_ps[:, k * P:(k + 1) * P], attn[:, r % 2, k * P:(k + 1) * P],
                                              ident[:, :])
                    last_t.then_inc(t_ready, 1)
                r = i - LAG_U

                def times_x(k0, k1, r=r):
                    b, gb = (r % TPH) // QT, (r // GT) % 2
                    for k in range((r % GT) * PER + k0, (r % GT) * PER + k1):
                        last_u = three(u_ps[:, :], xk_hi[:, b * KT + k, :], xk_lo[:, b * KT + k, :],
                                       at_hi[:, gb, k, :], at_lo[:, gb, k, :],
                                       start=(k == 0), stop=(k == KT - 1))
                    return last_u

                if exists(h, r, first) and r < TPH:
                    g, j = GPH * h + r // GT, r % GT
                    if first and r == 0:
                        pe.wait_ge(xk_split, B)
                    if j == 0:
                        pe.wait_ge(at_split, GT * (g + 1))
                        need(pe, u_split, g)
                    times_x(0, PER // 2)
                put_in = [i == AT_QB[0] and not tail, i == AT_QA[0] and not last, i == AT_WP and not tail,
                          i == AT_M and not last]
                if any(put_in):
                    pe.wait_ge(prob_ready, 2 * t + 1)
                if put_in[0]:
                    q_product(h, "b", (0,))
                if put_in[1]:
                    q_product(h + 1, "a", (0,))
                if put_in[2]:
                    for m in range(2):
                        last_w = pe.matmul(ring[0][:, 0:D], wv_s[:, m, :], wot_s[:, m, :],
                                           start=(m == 0), stop=(m == 1))
                    last_w.then_inc(wp_ready, 1)
                if put_in[3]:
                    m_product(h + 1)
                r = i - LAG_U
                if exists(h, r, first) and r < TPH:
                    last_u = times_x(PER // 2, PER)
                    if r % GT == GT - 1:
                        last_u.then_inc(u_ready, 1)
                r = i - LAG_O
                if exists(h, r, first) and r < TPH:
                    tt, j = t - LAG_O, r % GT
                    g = GPH * h + r // GT
                    if j == 0:
                        pe.wait_ge(u_split, g + 1)
                    if r == 0:
                        pe.wait_ge(ww_installed, 2 * (h + 1))
                    if not tail:
                        need(pe, y_added, tt)
                    elif i == TPH:
                        pe.wait_ge(prob_ready, 2 * H * TPH)
                    elif i >= TPH + 4:
                        pe.wait_ge(y_added, tt - 3)
                    q = slice(j * P, (j + 1) * P)
                    three(o_bank(r, last)[:, 0:WWN], u_hi[:, q], u_lo[:, q],
                          ww_hi[:, :], ww_lo[:, :]).then_inc(o_ready, 1)
                put_in = [i == AT_QB[1] and not tail, i == AT_QA[1] and not last, i == AT_WT and not tail]
                if any(put_in):
                    pe.wait_ge(prob_ready, 2 * t + 2)
                if put_in[0]:
                    q_product(h, "b", (1,))
                if put_in[1]:
                    q_product(h + 1, "a", (1,))
                if put_in[2]:
                    pe.wait_ge(vo_in, 32 * (h + 1))
                    for m in range(2):
                        pe.transpose(ring[1][:, m * P:(m + 1) * P], wv_s[:, m, :], ident[:, :])
                    for m in range(2):
                        last_w = pe.transpose(ring[1][:, NC + m * P:NC + (m + 1) * P], wo_s[:, m * P:(m + 1) * P],
                                              ident[:, :])
                    last_w.then_inc(wt_ready, 1)

            heads(pe, slot)

            pe.wait_ge(gate_in, 16)
            for b in range(B):
                pe.wait_ge(ln_done, b + 1)
                for j in range(QT):
                    last_t = pe.transpose(x1t_ps[b][:, j * P:(j + 1) * P], x1[:, b * QT + j, :], ident[:, :])
                last_t.then_inc(x1t_ready, 1)
                pe.wait_ge(x1t_copied, b + 1)
                for j in range(QT):
                    last_g = pe.matmul(o_ps[:, j * R + b * E:j * R + (b + 1) * E],
                                       acc_t[:, b * N + j * P:b * N + (j + 1) * P], gate_s[:, :],
                                       start=True, stop=True)
            last_g.then_inc(gate_ready, 1)
            pe.wait_ge(gate_step, 5)
            for j in range(QT):
                last_r = pe.transpose(t_ps[:, j * P:(j + 1) * P], pr_rep[:, j * P:(j + 1) * P], ident[:, :])
            last_r.then_inc(rows_ready, 1)
            pe.wait_ge(topk_const, 6)
            with pe.Fori(0, LEVELS // LEVELS_PT) as turn:
                for k in range(LEVELS_PT):
                    pe.wait_ge(hit_ready, LEVELS_PT * turn + k + 1)
                    pe.matmul(u_ps[:, 0:1], grp[:, :], hit[:, :], start=True, stop=True).then_inc(votes_ready, 1)
            pe.wait_ge(tie_step, 8)
            for j in range(QT):
                last_t = pe.transpose(t_ps[:, j * P:(j + 1) * P], cum[:, j * P:(j + 1) * P], ident[:, :])
            last_t.then_inc(slot_tok_ready, 1)

            def gather(e):
                for b in range(B):
                    pe.wait_ge(gat_ready, 2 * e + b + 1)
                    for part, (dst, src) in enumerate(((u_ps, x1_hi), (o_ps, x1_lo))):
                        if b == 0 and part == 0 and not is_at(e, 0):
                            pe.wait_ge(xs_copied, 2 * e)
                        for j in range(QT):
                            last_x = pe.matmul(dst[:, b * CAP:(b + 1) * CAP], src[:, b * QT + j, :],
                                               gat[:, b, j, :], start=(j == 0), stop=(j == QT - 1))
                    last_x.then_inc(xs_ready, 1)

            def up(e):
                pe.wait_ge(w1_split, e + 1)
                pe.wait_ge(xs_copied, 2 * (e + 1))
                for f in range(FT):
                    if f == 0:
                        need(pe, gelu_ready, FT * e)
                    elif f == 2:
                        need(pe, yt_copied, e)
                    elif f == 3:
                        pe.wait_ge(gelu_ready, FT * e + 1)
                    three(up_bank(f), w1_hi[:, f, :], w1_lo[:, f, :],
                          xs_hi[:, :], xs_lo[:, :]).then_inc(up_ready, 1)

            def down(e):
                pe.wait_ge(w2_split, e + 1)
                pe.wait_ge(gelu_ready, FT * e + 3)
                for f in range(FT):
                    if f < FD:
                        pe.wait_ge(g_split, FD * e + f + 1)
                    else:
                        pe.wait_ge(g_split_p, (FT - FD) * e + f - FD + 1)
                    last_d = three(t_ps[:, 0:SL], w2_hi[:, f, :], w2_lo[:, f, :], g_hi[:, f, :], g_lo[:, f, :],
                                   start=(f == 0), stop=(f == FT - 1))
                last_d.then_inc(down_ready, 1)

            def y_slots(e):
                pe.wait_ge(yt_copied, e + 1)
                need(pe, y_split, e)
                for j in range(B * CT):
                    last_t = pe.transpose(t_ps[:, NC + j * P:NC + (j + 1) * P], yt[:, j * P:(j + 1) * P],
                                          ident[:, :])
                last_t.then_inc(y_ready, 1)

            def scatter(e, ks=range(B * NCH)):
                pe.wait_ge(y_split, e + 1)
                for k in ks:
                    n, b, c = B * NCH * e + k, k // NCH, k % NCH
                    if c == 0:
                        pe.wait_ge(sca_ready, 2 * e + b + 1)
                    need(pe, prod_ready, n - 1)
                    for j in range(CT):
                        for part, y_part in enumerate(y_parts(e)):
                            last_o = pe.matmul(ring[1][:, (k % 2) * NC:(k % 2 + 1) * NC], y_part[:, b * CT + j, :],
                                               sca_of(e)[:, b, j, c * NC:(c + 1) * NC],
                                               start=(j == 0 and part == 0), stop=(j == CT - 1 and part == 1))
                    last_o.then_inc(out_ready, 1)

            pe.wait_ge(x1_split, B)
            gather(0)

            def ffn(e, first, tail):
                if not tail:
                    up(e)
                    if not is_at(e, E - 1):
                        gather(e + 1)
                    down(e)
                if is_at(e, E - 1):
                    scatter(e - 1, range(NCH))
                    y_slots(e)
                    scatter(e - 1, range(NCH, B * NCH))
                    return
                if not first:
                    scatter(e - 1)
                if not tail:
                    y_slots(e)

            experts(pe, ffn)
            for b in range(B):
                pe.wait_ge(acc_added, B * NCH * (E - 1) + b + 1)
                pe.wait_ge(acc_added_dve, b + 1)
                for j in range(QT):
                    last_t = pe.transpose(ring[b][:, j * P:(j + 1) * P],
                                          acc_t[:, b * N + j * P:b * N + (j + 1) * P], ident[:, :])
                last_t.then_inc(back_ready, 1)


_INS = ["L0_attn_X", "L0_attn_Wq", "L0_attn_Wk", "L0_attn_Wv", "L0_attn_Wo", "L0_attn_lambda_q1",
        "L0_attn_lambda_k1", "L0_attn_lambda_q2", "L0_attn_lambda_k2", "L0_attn_rms_scale",
        "L0_ffn_gate_w", "L0_ffn_w1", "L0_ffn_w2"]


def kernel(**inputs):
    import numpy as np
    import concourse.bacc as bacc
    from concourse.bass_utils import run_bass_kernel_spmd

    nc = bacc.Bacc("TRN2", target_bir_lowering=False, num_devices=1)
    arrays, args = {}, []
    for name in _INS:
        a = np.ascontiguousarray(inputs[name])
        arrays[f"in_{name}"] = a
        args.append(nc.dram_tensor(f"in_{name}", a.shape, mybir.dt.from_np(a.dtype), kind="ExternalInput").ap())
    shape = inputs["L0_attn_X"].shape
    out = nc.dram_tensor("out_x", shape, F32, kind="ExternalOutput").ap()
    build(nc, *args, out)
    r = run_bass_kernel_spmd(nc, [arrays], core_ids=[0])
    return r.results[0]["out_x"]
```
